# Optimizing a Trainium2 kernel written in Bass

```python
import numpy as np
import jax
import jax.numpy as jnp

def _softmax(x, axis=-1):
    return jax.nn.softmax(x, axis=axis)

def _gelu(x):
    return jax.nn.gelu(x, approximate=True)

def _silu(x):
    return jax.nn.silu(x)

def _sigmoid(x):
    return jax.nn.sigmoid(x)

def _layernorm(x, axis=-1, eps=1e-05):
    m = jnp.mean(x, axis=axis, keepdims=True)
    v = jnp.var(x, axis=axis, keepdims=True)
    return (x - m) / jnp.sqrt(v + eps)

def _scatter_add(tgt, idx, src, axis=0):
    return tgt.at[idx].add(src)

def _segment_sum(src, seg, n):
    return jax.ops.segment_sum(src, seg, n)
kernel_name = 'mk_macaron_d1_jaxref_r8_aa2826'

def setup_inputs(seed: int=0):
    np.random.seed(seed)
    _w = jnp.asarray

    def _L0_attn_setup():
        import jax, jax.numpy as jnp
        import numpy as np
        from math import sqrt
        ROPE_BASE = 6000.0

        def _rope_tables(seq_len, rope_dim, dtype):
            inv_freq = 1.0 / ROPE_BASE ** (jnp.arange(0, rope_dim, 2, dtype=jnp.float32) / rope_dim)
            t = jnp.arange(seq_len, dtype=jnp.float32)
            freqs = jnp.outer(t, inv_freq)
            emb = jnp.concatenate([freqs, freqs], axis=-1)
            return (jnp.cos(emb).astype(dtype), jnp.sin(emb).astype(dtype))

        def _rotate_half(x):
            x1, x2 = jnp.split(x, 2, axis=-1)
            return jnp.concatenate([-x2, x1], axis=-1)
        key = jax.random.key(seed)
        k1, k2, k3 = jax.random.split(key, 3)
        B, S, D = (2, 256, 128)
        H, DK = (16, 64)
        x = jax.random.normal(k1, (B, S, D), dtype=jnp.float32)
        W_qkv = jax.random.normal(k2, (3, H, DK, D), dtype=jnp.float32) * 0.02
        W_o = jax.random.normal(k3, (D, H * DK), dtype=jnp.float32) * 0.02
        return {'x': x, 'W_qkv': W_qkv, 'W_o': W_o}
    _L0_attn_in = _L0_attn_setup()

    def _L0_ffn_setup():
        import jax, jax.numpy as jnp
        import numpy as np
        B, S, D, H, DOUT, E, K = (4, 256, 128, 128, 128, 8, 2)
        key = jax.random.key(seed)
        k1, k2, k3, k4 = jax.random.split(key, 4)
        x = jax.random.normal(k1, (B, S, D), dtype=jnp.float32)
        Wr = jax.random.normal(k2, (D, E), dtype=jnp.float32) * 0.02
        Wi = jax.random.normal(k3, (E, D, H), dtype=jnp.float32) * 0.02
        Wo = jax.random.normal(k4, (E, H, DOUT), dtype=jnp.float32) * 0.02
        return {'x': x, 'Wr': Wr, 'Wi': Wi, 'Wo': Wo}
    _L0_ffn_in = _L0_ffn_setup()
    _d = {'L0_attn_x': _L0_attn_in['x'], 'L0_attn_W_qkv': _L0_attn_in['W_qkv'], 'L0_attn_W_o': _L0_attn_in['W_o'], 'L0_ffn_Wr': _L0_ffn_in['Wr'], 'L0_ffn_Wi': _L0_ffn_in['Wi'], 'L0_ffn_Wo': _L0_ffn_in['Wo']}
    _x0 = _d['L0_attn_x']
    _d['L0_attn_x'] = jax.random.normal(jax.random.fold_in(jax.random.key(seed), 1), (16, 512, 128), dtype=_x0.dtype)
    del _x0
    return _d

def reference(L0_attn_x, L0_attn_W_qkv, L0_attn_W_o, L0_ffn_Wr, L0_ffn_Wi, L0_ffn_Wo):

    def _L0_attn_ref(x, W_qkv, W_o):
        import jax, jax.numpy as jnp
        import numpy as np
        from math import sqrt
        ROPE_BASE = 6000.0

        def _rope_tables(seq_len, rope_dim, dtype):
            inv_freq = 1.0 / ROPE_BASE ** (jnp.arange(0, rope_dim, 2, dtype=jnp.float32) / rope_dim)
            t = jnp.arange(seq_len, dtype=jnp.float32)
            freqs = jnp.outer(t, inv_freq)
            emb = jnp.concatenate([freqs, freqs], axis=-1)
            return (jnp.cos(emb).astype(dtype), jnp.sin(emb).astype(dtype))

        def _rotate_half(x):
            x1, x2 = jnp.split(x, 2, axis=-1)
            return jnp.concatenate([-x2, x1], axis=-1)
        B, S, D = x.shape
        _, H, DK, _ = W_qkv.shape
        rope_dim = DK // 2
        qkv = jnp.einsum('bsm,qhdm->bqhsd', x, W_qkv)
        cos, sin = _rope_tables(S, rope_dim, x.dtype)
        qk = qkv[:, :2, :, :, :rope_dim]
        qk_rot = qk * cos + _rotate_half(qk) * sin
        qkv = qkv.at[:, :2, :, :, :rope_dim].set(qk_rot)
        Q, K, V = (qkv[:, 0], qkv[:, 1], qkv[:, 2])
        scores = jnp.einsum('bhqd,bhkd->bhqk', Q, K)
        causal = jnp.triu(jnp.ones((S, S), dtype=bool), k=1)
        scores = jnp.where(causal, -jnp.inf, scores) / sqrt(DK)
        attn = jax.nn.softmax(scores, axis=-1)
        out = jnp.einsum('bhqk,bhkd->bhqd', attn, V)
        out = out.transpose(0, 2, 1, 3).reshape(B, S, H * DK)
        return jnp.einsum('bsh,dh->bsd', out, W_o)

    def _L0_ffn_ref(x, Wr, Wi, Wo):
        import jax, jax.numpy as jnp
        import numpy as np
        B, S, D, H, DOUT, E, K = (4, 256, 128, 128, 128, 8, 2)
        b, s, d = x.shape
        e_cnt, _, h = Wi.shape
        dout = Wo.shape[2]
        xf = x.reshape(-1, d)
        T = xf.shape[0]
        probs = jax.nn.softmax(xf @ Wr, axis=-1)
        topk_p, topk_i = jax.lax.top_k(probs, K)
        mask = topk_i[:, :, None] == jnp.arange(e_cnt)[None, None, :]
        hmix = jnp.zeros((T, K, h), dtype=xf.dtype)
        for e in range(e_cnt):
            he = xf @ Wi[e]
            hmix = hmix + jnp.where(mask[:, :, e][:, :, None], he[:, None, :], 0.0)
        o = jnp.zeros((T, K, dout), dtype=xf.dtype)
        for e in range(e_cnt):
            oe = jnp.einsum('tkh,hd->tkd', hmix, Wo[e])
            o = o + jnp.where(mask[:, :, e][:, :, None], oe, 0.0)
        out = jnp.sum(o * topk_p[:, :, None], axis=1)
        return out.reshape(b, s, dout)
    x = L0_attn_x
    x = x + 0.5 * _L0_ffn_ref(_layernorm(x, axis=-1), L0_ffn_Wr, L0_ffn_Wi, L0_ffn_Wo)
    x = x + _L0_attn_ref(_layernorm(x, axis=-1), L0_attn_W_qkv, L0_attn_W_o)
    x = x + 0.5 * _L0_ffn_ref(_layernorm(x, axis=-1), L0_ffn_Wr, L0_ffn_Wi, L0_ffn_Wo)
    return x

_drawn_inputs = setup_inputs


def setup_inputs(seed=0):
    import zlib

    import numpy as np

    out = dict(_drawn_inputs(seed))
    spreads = {}
    factors = {'L0_attn_W_qkv': 3.395,
     'L0_attn_W_o': 3.444,
     'L0_ffn_Wr': 5.525,
     'L0_ffn_Wi': 4.832,
     'L0_ffn_Wo': 4.82}
    for name, (base, spread) in spreads.items():
        noise = np.random.default_rng([zlib.crc32(name.encode()), seed]).standard_normal(out[name].shape)
        drawn = base * np.exp(spread * noise) if base else spread * noise
        out[name] = jnp.asarray(drawn.astype(out[name].dtype))
    for name, factor in factors.items():
        out[name] = (out[name] * factor).astype(out[name].dtype)
    return out
```

```python
import concourse.bass as bass
from concourse import mybir
from contextlib import ExitStack
import numpy as np

F32 = mybir.dt.float32
F32R = mybir.dt.float32r
BF16 = mybir.dt.bfloat16
ALU = mybir.AluOpType
ACT = mybir.ActivationFunctionType
AX = mybir.AxisListType

P = 128
B, S, D = 16, 512, 128
H, DK = 16, 64
E = 8
TOPK = 2
EPS = 1e-5
ROPE = DK // 2
QT = S // P
NPAIR = H // 2
BANK = 512

SCORE_AT = {3: (0, 0), 2: (1, 512), 0: (1, 896), 1: (2, 1024)}
SCORE_UNITS = [[3], [2, 0], [1]]
PROBT_AT = {0: (0, 0), 1: (1, 512), 3: (1, 896), 2: (2, 1024)}
PROBT_UNITS = [[0], [1, 3], [2]]
PROB_COLS = 1280


def order_of_misc_banks():
    units = [("T", 0, 0)] + [("V", 0, j) for j in range(QT)]
    units += [(k, 0, p) for p in (0, 1) for k in ("Qm", "Qr", "Km", "Kr")]
    for b in range(B):
        for p in range(NPAIR):
            if (b, p) > (0, 0):
                units.append(("R",) + ((b, p - 1) if p else (b - 1, NPAIR - 1)))
            nb, np_ = (b, p + 2) if p + 2 < NPAIR else (b + 1, p + 2 - NPAIR)
            if nb < B:
                units += [(k, nb, np_) for k in ("Qm", "Qr", "Km", "Kr")]
            if p == 0:
                units += [("V", b, QT + j) for j in range(QT)]
                if b:
                    units.append(("O", b - 1, 0))
            if p == 5 and b + 1 < B:
                units.append(("T", b + 1, 0))
            if p == 7 and b + 1 < B:
                units += [("V", b + 1, j) for j in range(QT)]
    return units + [("R", B - 1, NPAIR - 1), ("O", B - 1, 0)]


class Misc:

    def __init__(self):
        self.units = order_of_misc_banks()
        self.at = {u: n for n, u in enumerate(self.units)}
        self.reader = ["act" if u[0] in ("V", "R") else "dve" for u in self.units]
        self.read = {"act": [], "dve": []}
        for r in self.reader:
            for k in self.read:
                self.read[k].append((self.read[k][-1] if self.read[k] else 0) + (r == k))

    def linear(self, value, unit):
        kind, (i, shift), index = unit
        if isinstance(i, int):
            return value(self.at[(kind, i + shift, index)])
        mid = 5
        a, b = (value(self.at[(kind, m + shift, index)]) for m in (mid, mid + 1))
        return i * (b - a) + (a - mid * (b - a))

    def bank(self, unit):
        kind, (i, shift), index = unit
        return self.at[(kind, (i if isinstance(i, int) else 5) + shift, index)] % 2

    def ready(self, unit):
        return self.linear(lambda n: n + 1, unit)

    def free(self, unit):
        kind, (i, shift), index = unit
        n = self.at[(kind, (i if isinstance(i, int) else 5) + shift, index)]
        if n < 2:
            return None
        who = self.reader[n - 2]
        return who, self.linear(lambda m: self.read[who][m - 2], unit)


def build(nc, x, w_qkv, w_o, w_r, w_i, w_out, cos_q, sin_q, cos_k, sin_k, ident_d, rank_d, mask_d, out):
    outer = ExitStack()
    with outer:
        def sb(name, shape, dt=F32, stack=outer):
            return stack.enter_context(nc.sbuf_tensor(name, shape, dt))

        def sem(name, stack=outer):
            return stack.enter_context(nc.semaphore(name))

        X = sb("X", [P, B * QT, D])
        W_hi = sb("W_hi", [P, 5, H * DK], F32R)
        W_lo = sb("W_lo", [P, 5, H * DK], F32R)
        WoT = sb("WoT", [P, NPAIR, D])
        M_hi = sb("M_hi", [P, E * D], F32R)
        M_lo = sb("M_lo", [P, E * D], F32R)
        Wr_hi = sb("Wr_hi", [P, E], F32R)
        Wr_lo = sb("Wr_lo", [P, E], F32R)
        tables = sb("tables", [P, 4, S])
        ident = sb("ident", [P, P])
        ident_b = sb("ident_b", [P, P], BF16)
        mask_b = sb("mask_b", [P, P], BF16)
        ranks = sb("ranks", [P, 2, E, E])
        minus_half = sb("minus_half", [P, QT])
        stats = sb("stats", [P, QT, 6])
        meanvar = sb("meanvar", [P, QT, 2])
        var_eps = sb("var_eps", [P, QT])
        rstd = sb("rstd", [P, QT])
        carrier = sb("carrier", [P, 1])
        xn = sb("xn", [P, QT, D])
        banks = outer.enter_context(nc.psum_tensor("banks", [P, 8, BANK], F32))
        flat = banks[:, :, :].rearrange("p a b -> p (a b)")

        with ExitStack() as st:
            wn = sb("wn", [P, 24, P], stack=st)
            won = sb("won", [P, H * DK], stack=st)
            win = sb("win", [P, E, P], stack=st)
            wit = sb("wit", [P, E, P], stack=st)
            woutn = sb("woutn", [P, E, P], stack=st)
            wrn = sb("wrn", [P, E], stack=st)
            mask_f = sb("mask_f", [P, P], stack=st)
            x_in, const_in, w_in, wo_in, wi_in, wout_in = (sem(n, st) for n in (
                "x_in", "const_in", "w_in", "wo_in", "wi_in", "wout_in"))
            turned, hi_done, lo_done, rolled, prod_ready, filled = (sem(n, st) for n in (
                "turned", "hi_done", "lo_done", "rolled", "prod_ready", "filled"))
            NW = 6
            with nc.Block() as block:

                @block.sync
                def _(sp):
                    sp.dma_start(ident[:, :], ident_d).then_inc(const_in, 16)
                    sp.dma_start(wn[:, :, :], w_qkv.rearrange("q h d m -> (q h d) m").rearrange(
                        "(t p) m -> p t m", p=P)).then_inc(w_in, 16)
                    sp.dma_start(won[:, :], w_o).then_inc(wo_in, 16)
                    sp.dma_start(X[:, 0:32, :], x.rearrange("b (t p) d -> p (b t) d", p=P)[:, 0:32, :]).then_inc(x_in, 16)
                    sp.wait_ge(x_in, 32)

                @block.scalar
                def _(act):
                    act.dma_start(win[:, :, :], w_i.rearrange("e d h -> d e h")).then_inc(wi_in, 16)
                    act.dma_start(woutn[:, :, :], w_out.rearrange("e h d -> h e d")).then_inc(wout_in, 16)
                    act.dma_start(wrn[:, :], w_r).then_inc(const_in, 16)
                    act.dma_start(mask_f[:, :], mask_d).then_inc(const_in, 16)
                    act.dma_start(ranks[:, :, :, :], rank_d).then_inc(const_in, 16)
                    for n, t in enumerate((cos_q, sin_q, cos_k, sin_k)):
                        act.dma_start(tables[:, n, :], t).then_inc(const_in, 16)
                    act.dma_start(X[:, 32:64, :], x.rearrange("b (t p) d -> p (b t) d", p=P)[:, 32:64, :]).then_inc(x_in, 16)
                    for g in range(NW):
                        act.wait_ge(turned, g + 1)
                        act.activation(W_hi[:, g // 2, (g % 2) * BANK:(g % 2 + 1) * BANK], banks[:, g, :],
                                       ACT.Copy).then_inc(hi_done, 1)
                    for g in range(2):
                        act.wait_ge(turned, NW + g + 1)
                        act.activation(WoT[:, 4 * g:4 * g + 4, :], banks[:, 6 + g, :].rearrange("p (a b) -> p a b", a=4),
                                       ACT.Copy).then_inc(hi_done, 1)
                    for g in range(2):
                        act.wait_ge(turned, NW + 2 + g + 1)
                        act.activation(wit[:, 4 * g:4 * g + 4, :], banks[:, g, :].rearrange("p (a b) -> p a b", a=4),
                                       ACT.Copy).then_inc(hi_done, 1)
                    for g in range(2):
                        act.wait_ge(prod_ready, g + 1)
                        act.activation(M_hi[:, g * BANK:(g + 1) * BANK], banks[:, 2 + g, :], ACT.Copy).then_inc(hi_done, 1)
                    act.wait_ge(const_in, 16 * 8)
                    act.activation(Wr_hi[:, :], wrn[:, :], ACT.Copy).then_inc(hi_done, 1)

                @block.tensor
                def _(pe):
                    pe.wait_ge(const_in, 16 * 8)
                    pe.wait_ge(w_in, 16)
                    for g in range(NW):
                        for a in range(4):
                            mm = pe.transpose(banks[:, g, a * P:(a + 1) * P], wn[:, 4 * g + a, :], ident[:, :])
                        mm.then_inc(turned, 1)
                    pe.wait_ge(wo_in, 16)
                    for g in range(2):
                        for a in range(4):
                            mm = pe.transpose(banks[:, 6 + g, a * P:(a + 1) * P],
                                              won[:, (4 * g + a) * P:(4 * g + a + 1) * P], ident[:, :])
                        mm.then_inc(turned, 1)
                    pe.wait_ge(wi_in, 16)
                    for g in range(2):
                        pe.wait_ge(lo_done, g + 1)
                        for a in range(4):
                            mm = pe.transpose(banks[:, g, a * P:(a + 1) * P], win[:, 4 * g + a, :], ident[:, :])
                        mm.then_inc(turned, 1)
                    pe.wait_ge(wout_in, 16)
                    pe.wait_ge(hi_done, NW + 4)
                    pe.wait_ge(lo_done, 4)
                    for g in range(2):
                        for a in range(4):
                            e = 4 * g + a
                            mm = pe.matmul(banks[:, 2 + g, a * P:(a + 1) * P], wit[:, e, :], woutn[:, e, :],
                                           start=True, stop=True)
                        mm.then_inc(prod_ready, 1)

                @block.vector
                def _(dve):
                    dve.memset(W_hi[:, 3:5, :].bitcast(F32), 0.0).then_inc(filled, 1)
                    dve.memset(W_lo[:, 3:5, :].bitcast(F32), 0.0).then_inc(filled, 1)
                    dve.memset(minus_half[:, :], -0.5)
                    for g in range(NW):
                        dve.wait_ge(hi_done, g + 1)
                        cols = slice((g % 2) * BANK, (g % 2 + 1) * BANK)
                        dve.tensor_tensor(W_lo[:, g // 2, cols], banks[:, g, :], W_hi[:, g // 2, cols].bitcast(F32),
                                          ALU.subtract).then_inc(lo_done, 1)
                    dve.wait_ge(filled, 2)
                    dve.wait_ge(lo_done, 4)
                    for w in (W_hi, W_lo):
                        for q in range(2):
                            src = w[:, q, :].rearrange("p (h d) -> p h d", d=DK)
                            dst = w[:, 3 + q, :].rearrange("p (h d) -> p h d", d=DK)
                            half = ROPE // 2
                            dve.tensor_copy(dst[:, :, 0:half], src[:, :, half:ROPE]).then_inc(rolled, 1)
                            dve.tensor_copy(dst[:, :, half:ROPE], src[:, :, 0:half]).then_inc(rolled, 1)
                    for g in range(2):
                        dve.wait_ge(hi_done, NW + 4 + g + 1)
                        cols = slice(g * BANK, (g + 1) * BANK)
                        dve.tensor_tensor(M_lo[:, cols], banks[:, 2 + g, :], M_hi[:, cols].bitcast(F32),
                                          ALU.subtract).then_inc(lo_done, 1)
                    dve.wait_ge(hi_done, NW + 7)
                    dve.tensor_tensor(Wr_lo[:, :], wrn[:, :], Wr_hi[:, :].bitcast(F32), ALU.subtract).then_inc(lo_done, 1)
                    dve.wait_ge(const_in, 16 * 8)
                    dve.tensor_copy(ident_b[:, :], ident[:, :]).then_inc(rolled, 1)
                    dve.tensor_copy(mask_b[:, :], mask_f[:, :]).then_inc(rolled, 1)
                    dve.wait_ge(rolled, 10)

        stats_done, agg_done, eps_done, rstd_done, xn_done = (
            sem(n) for n in ("stats_done", "agg_done", "eps_done", "rstd_done", "xn_done"))
        LN_RUNS = {"ffn1": 0, "attn": B, "ffn2": 2 * B}

        def norm_stats(dve, n, run):
            k = n + LN_RUNS[run]
            for i in range(QT):
                st = dve.bn_stats(stats[:, i, :], X[:, n * QT + i, :])
            st.then_inc(stats_done, 1)
            dve.wait_ge(stats_done, k + 1)
            dve.memset(carrier[:, :], 0.0)
            for i in range(QT):
                st = dve.bn_aggr(meanvar[:, i, :], stats[:, i, :])
            st.then_inc(agg_done, 1)
            dve.wait_ge(agg_done, k + 1)
            dve.tensor_scalar(var_eps[:, :], meanvar[:, :, 1], EPS, None, ALU.add).then_inc(eps_done, 1)

        def norm_rstd(pool, n, run):
            k = n + LN_RUNS[run]
            pool.wait_ge(eps_done, k + 1)
            pool.tensor_tensor(rstd[:, :], var_eps[:, :], minus_half[:, :], ALU.pow).then_inc(rstd_done, 1)

        def norm_apply(dve, n, run):
            k = n + LN_RUNS[run]
            dve.wait_ge(rstd_done, k + 1)
            for i in range(QT):
                st = dve.tensor_scalar(xn[:, i, :], X[:, n * QT + i, :], meanvar[:, i, 0:1], rstd[:, i:i + 1],
                                       ALU.subtract, ALU.mult)
            st.then_inc(xn_done, 1)

        def ffn(run, last_phase):
            with ExitStack() as st:
                def fsb(name, shape, dt=F32):
                    return sb(f"{name}_{run}", shape, dt, st)

                def fsem(name):
                    return sem(f"{name}_{run}", st)

                xT_hi = fsb("xT_hi", [P, 2, S], F32R)
                xT_lo = fsb("xT_lo", [P, 2, S], F32R)
                logit = fsb("logit", [P, QT, E])
                top = fsb("top", [P, QT])
                shifted = fsb("shifted", [P, QT, E])
                expo = fsb("expo", [P, QT, E])
                total = fsb("total", [P, QT])
                inv_total = fsb("inv_total", [P, QT])
                gt = fsb("gt", [P, QT, E, E])
                ge = fsb("ge", [P, QT, E, E])
                rank = fsb("rank", [P, QT, E])
                taken = fsb("taken", [P, QT, E])
                chosen = fsb("chosen", [P, QT, E])
                gate = fsb("gate", [P, 2, QT, E])
                Z = fsb("Z", [P, 2, E, D])
                xT_ready, hi_ready, lo_ready, logit_ready, logit_copied, y_ready, z_ready, summed, adds = (
                    fsem(n) for n in ("xT_ready", "hi_ready", "lo_ready", "logit_ready", "logit_copied",
                                      "y_ready", "z_ready", "summed", "adds"))
                shift_ready, expo_ready, gate_ready, g_top, g_cmp, g_mul, g_add, g_rank, g_take, g_tot, g_inv, g_pick = (
                    fsem(n) for n in ("shift_ready", "expo_ready", "gate_ready", "g_top", "g_cmp", "g_mul", "g_add",
                                      "g_rank", "g_take", "g_tot", "g_inv", "g_pick"))
                out_done = fsem("out_done")
                T_BANK, L_BANK, Y_BANK = 0, 1, 2

                with nc.Block() as block:

                    @block.tensor
                    def _(pe):
                        def turn(n, k, start=False):
                            pe.wait_ge(xn_done, n + LN_RUNS[run] + 1)
                            if not start:
                                pe.wait_ge(lo_ready, n)
                            for i in range(QT):
                                mm = pe.transpose(banks[:, T_BANK, i * P:(i + 1) * P], xn[:, i, :], ident[:, :])
                            mm.then_inc(xT_ready, 1)

                        def logits(n, k, start=False):
                            pe.wait_ge(lo_ready, n + 1)
                            if not start:
                                pe.wait_ge(logit_copied, n)
                            for i in range(QT):
                                tok = slice(i * P, (i + 1) * P)
                                o = banks[:, L_BANK, i * E:(i + 1) * E]
                                pe.matmul(o, xT_hi[:, k, tok], Wr_hi[:, :], start=True, stop=False)
                                pe.matmul(o, xT_hi[:, k, tok], Wr_lo[:, :], start=False, stop=False)
                                mm = pe.matmul(o, xT_lo[:, k, tok], Wr_hi[:, :], start=False, stop=True)
                            mm.then_inc(logit_ready, 1)

                        def experts(n, k, i, start=False):
                            if not (start and i < 2):
                                pe.wait_ge(z_ready, n * QT + i - 1)
                            tok = slice(i * P, (i + 1) * P)
                            for c in range(2):
                                o = banks[:, Y_BANK + 2 * (i % 2) + c, :]
                                cols = slice(c * BANK, (c + 1) * BANK)
                                pe.matmul(o, xT_hi[:, k, tok], M_hi[:, cols], start=True, stop=False)
                                pe.matmul(o, xT_hi[:, k, tok], M_lo[:, cols], start=False, stop=False)
                                mm = pe.matmul(o, xT_lo[:, k, tok], M_hi[:, cols], start=False, stop=True)
                            mm.then_inc(y_ready, 1)

                        def step(n, k, more, start=False):
                            experts(n, k, 0, start)
                            experts(n, k, 1, start)
                            if more:
                                turn(n + 1, 1 - k)
                            experts(n, k, 2)
                            if more:
                                logits(n + 1, 1 - k)
                            experts(n, k, 3)

                        turn(0, 0, True)
                        logits(0, 0, True)
                        step(0, 0, True, True)
                        step(1, 1, True)
                        with pe.Fori(1, B // 2 - 1) as j:
                            step(j * 2, 0, True)
                            step(j * 2 + 1, 1, True)
                        step(B - 2, 0, True)
                        step(B - 1, 1, False)

                    @block.scalar
                    def _(act):
                        def split(n, k, start=False):
                            act.wait_ge(xT_ready, n + 1)
                            if not start:
                                act.wait_ge(y_ready, n * QT - QT)
                            act.activation(xT_hi[:, k, :], banks[:, T_BANK, :], ACT.Copy).then_inc(hi_ready, 1)

                        def routing(n, k):
                            act.wait_ge(logit_ready, n + 1)
                            act.activation(logit[:, :, :], banks[:, L_BANK, 0:QT * E].rearrange("p (t e) -> p t e", e=E),
                                           ACT.Copy).then_inc(logit_copied, 1)
                            act.wait_ge(shift_ready, n + 1)
                            act.activation(expo[:, :, :], shifted[:, :, :], ACT.Exp).then_inc(expo_ready, 1)

                        split(0, 0, True)
                        routing(0, 0)
                        split(1, 1, True)
                        routing(1, 1)
                        with act.Fori(1, B // 2) as j:
                            split(j * 2, 0)
                            routing(j * 2, 0)
                            split(j * 2 + 1, 1)
                            routing(j * 2 + 1, 1)

                    @block.vector
                    def _(dve):
                        def low(n, k):
                            dve.wait_ge(hi_ready, n + 1)
                            dve.tensor_tensor(xT_lo[:, k, :], banks[:, T_BANK, :], xT_hi[:, k, :].bitcast(F32),
                                              ALU.subtract).then_inc(lo_ready, 1)

                        def gates(n, k):
                            dve.wait_ge(logit_copied, n + 1)
                            dve.tensor_reduce(top[:, :], logit[:, :, :], AX.X, ALU.max).then_inc(g_top, 1)
                            by_e = logit[:, :, :].unsqueeze(3).broadcast_to([P, QT, E, E])
                            by_j = logit[:, :, :].unsqueeze(2).broadcast_to([P, QT, E, E])
                            for t in range(QT):
                                dve.tensor_tensor(gt[:, t], by_j[:, t], by_e[:, t], ALU.is_gt)
                                cmp = dve.tensor_tensor(ge[:, t], by_j[:, t], by_e[:, t], ALU.is_ge)
                            cmp.then_inc(g_cmp, 1)
                            dve.wait_ge(g_top, n + 1)
                            dve.tensor_tensor(shifted[:, :, :], logit[:, :, :],
                                              top[:, :].unsqueeze(2).broadcast_to([P, QT, E]),
                                              ALU.subtract).then_inc(shift_ready, 1)
                            dve.wait_ge(g_cmp, n + 1)
                            flat8 = lambda a: a.rearrange("p t e j -> p t (e j)")
                            after = ranks[:, 0].rearrange("p e j -> p (e j)").unsqueeze(1).broadcast_to([P, QT, E * E])
                            before = ranks[:, 1].rearrange("p e j -> p (e j)").unsqueeze(1).broadcast_to([P, QT, E * E])
                            dve.tensor_tensor(flat8(gt[:, :, :, :]), flat8(gt[:, :, :, :]), after, ALU.mult)
                            dve.tensor_tensor(flat8(ge[:, :, :, :]), flat8(ge[:, :, :, :]), before,
                                              ALU.mult).then_inc(g_mul, 1)
                            dve.wait_ge(g_mul, n + 1)
                            dve.tensor_tensor(flat8(gt[:, :, :, :]), flat8(gt[:, :, :, :]), flat8(ge[:, :, :, :]),
                                              ALU.add).then_inc(g_add, 1)
                            dve.wait_ge(g_add, n + 1)
                            dve.tensor_reduce(rank[:, :, :], gt[:, :, :, :], AX.X, ALU.add).then_inc(g_rank, 1)
                            dve.wait_ge(g_rank, n + 1)
                            dve.tensor_scalar(taken[:, :, :], rank[:, :, :], TOPK - 0.5, 0.5, ALU.is_lt,
                                              ALU.mult).then_inc(g_take, 1)
                            dve.wait_ge(expo_ready, n + 1)
                            dve.tensor_reduce(total[:, :], expo[:, :, :], AX.X, ALU.add).then_inc(g_tot, 1)
                            dve.wait_ge(g_take, n + 1)
                            dve.tensor_tensor(chosen[:, :, :], expo[:, :, :], taken[:, :, :], ALU.mult).then_inc(g_pick, 1)
                            dve.wait_ge(g_tot, n + 1)
                            dve.reciprocal(inv_total[:, :], total[:, :]).then_inc(g_inv, 1)
                            dve.wait_ge(g_inv, n + 1)
                            dve.wait_ge(g_pick, n + 1)
                            dve.tensor_tensor(gate[:, k, :, :], chosen[:, :, :],
                                              inv_total[:, :].unsqueeze(2).broadcast_to([P, QT, E]),
                                              ALU.mult).then_inc(gate_ready, 1)

                        def weigh(n, k, i, start=False):
                            if i == 0:
                                dve.wait_ge(gate_ready, n + 1)
                            dve.wait_ge(y_ready, n * QT + i + 1)
                            if not (start and i < 2):
                                dve.wait_ge(summed, n * QT + i - 1)
                            y = flat[:, (Y_BANK + 2 * (i % 2)) * BANK:(Y_BANK + 2 * (i % 2) + 2) * BANK]
                            dve.tensor_tensor(Z[:, i % 2, :, :], y.rearrange("p (e d) -> p e d", e=E),
                                              gate[:, k, i, :].unsqueeze(2).broadcast_to([P, E, D]),
                                              ALU.mult).then_inc(z_ready, 1)

                        def step(n, k, more, start=False):
                            weigh(n, k, 0, start)
                            if more:
                                norm_stats(dve, n + 1, run)
                            weigh(n, k, 1, start)
                            if more:
                                norm_apply(dve, n + 1, run)
                            weigh(n, k, 2)
                            if more:
                                low(n + 1, 1 - k)
                            weigh(n, k, 3)
                            if more:
                                gates(n + 1, 1 - k)

                        norm_stats(dve, 0, run)
                        norm_apply(dve, 0, run)
                        low(0, 0)
                        gates(0, 0)
                        step(0, 0, True, True)
                        step(1, 1, True)
                        with dve.Fori(1, B // 2 - 1) as j:
                            step(j * 2, 0, True)
                            step(j * 2 + 1, 1, True)
                        step(B - 2, 0, True)
                        step(B - 1, 1, False)

                    @block.gpsimd
                    def _(pool):
                        def add_up(n, i):
                            t = n * QT + i
                            z = Z[:, i % 2, :, :]
                            pool.wait_ge(z_ready, t + 1)
                            pool.tensor_tensor(z[:, 0:4], z[:, 0:4], z[:, 4:8], ALU.add).then_inc(adds, 1)
                            pool.wait_ge(adds, t * 3 + 1)
                            pool.tensor_tensor(z[:, 0:2], z[:, 0:2], z[:, 2:4], ALU.add).then_inc(adds, 1)
                            pool.wait_ge(adds, t * 3 + 2)
                            pool.tensor_tensor(z[:, 0], z[:, 0], z[:, 1], ALU.add).then_inc(adds, 1)
                            pool.wait_ge(adds, t * 3 + 3)
                            pool.tensor_tensor(X[:, t, :], X[:, t, :], z[:, 0], ALU.add).then_inc(summed, 1)

                        def step(n, more):
                            add_up(n, 0)
                            if more:
                                norm_rstd(pool, n + 1, run)
                            for i in range(1, QT):
                                add_up(n, i)

                        norm_rstd(pool, 0, run)
                        with pool.Fori(0, B - 1) as n:
                            step(n, True)
                        step(B - 1, False)

                    if last_phase:
                        @block.sync
                        def _(sp):
                            o = out.rearrange("b (t p) d -> p b t d", p=P)
                            with sp.Fori(0, B) as n:
                                sp.wait_ge(summed, n * QT + QT)
                                sp.dma_start(o[:, bass.ds(n, 1), :, :], X[:, bass.ds(n * QT, QT), :].rearrange(
                                    "p (a t) d -> p a t d", a=1)).then_inc(out_done, 16)
                            sp.wait_ge(out_done, 16 * B)

        def attention():
            with ExitStack() as st:
                def asb(name, shape, dt=F32):
                    return sb(name, shape, dt, st)

                def asem(name):
                    return sem(name, st)

                xT_hi = asb("xT_hi", [P, S], F32R)
                xT_lo = asb("xT_lo", [P, S], F32R)
                V = asb("V", [P, QT, H * DK])
                rot = asb("rot", [P, 4, S])
                Qp = asb("Qp", [P, 2, 2, S])
                Kp = asb("Kp", [P, 2, S])
                probs = asb("probs", [P, PROB_COLS])
                probsT = asb("probsT", [P, 2, PROB_COLS])
                negmax = asb("negmax", [P, 2, QT])
                den = asb("den", [P, 2, QT, 2])
                inv_den = asb("inv_den", [P, QT, 2])
                inv_wide = asb("inv_wide", [P, QT, P])
                R = asb("R", [P, S])
                OT = asb("OT", [P, NPAIR, S])
                misc_ready, misc_read_act, misc_read_dve, T_hi = (
                    asem(n) for n in ("misc_ready", "misc_read_act", "misc_read_dve", "T_hi"))
                padded, half_added, qk_ready, scores_ready, max_ready, exp_done = (
                    asem(n) for n in ("padded", "half_added", "qk_ready", "scores_ready", "max_ready", "exp_done"))
                pt_ready, pt_copied_act, pt_copied_dve, pv_ready, inv_done, inv_ready, o_ready = (
                    asem(n) for n in ("pt_ready", "pt_copied_act", "pt_copied_dve", "pv_ready", "inv_done",
                                      "inv_ready", "o_ready"))
                misc = Misc()
                MISC_BANK, PT_BANK, O_BANK = 3, 5, 7

                def head_no(b, shift, h):
                    return (b + shift) * H + h

                def pair_no(b, shift, p):
                    return (b + shift) * NPAIR + p

                def before(b, p, back):
                    return (0, p - back) if p >= back else (-1, p - back + NPAIR)

                def after(p, ahead):
                    return (0, p + ahead) if p + ahead < NPAIR else (1, p + ahead - NPAIR)

                def batches(engine, prologue, body, epilogue):
                    prologue()
                    body(0, True, False)
                    with engine.Fori(1, B - 1) as b:
                        body(b, False, False)
                    body(B - 1, False, True)
                    epilogue()

                with nc.Block() as block:

                    @block.tensor
                    def _(pe):
                        def claim(unit):
                            free = misc.free(unit)
                            if free:
                                pe.wait_ge(misc_read_act if free[0] == "act" else misc_read_dve, free[1])
                            return banks[:, MISC_BANK + misc.bank(unit), :]

                        def turn(b, sh):
                            o = claim(("T", (b, sh), 0))
                            pe.wait_ge(xn_done, b + sh + LN_RUNS["attn"] + 1)
                            for i in range(QT):
                                mm = pe.transpose(o[:, i * P:(i + 1) * P], xn[:, i, :], ident[:, :])
                            mm.then_inc(misc_ready, 1)

                        def split_product(o, l_hi, l_lo, r_hi, r_lo):
                            pe.matmul(o, l_hi, r_hi, start=True, stop=False)
                            pe.matmul(o, l_lo, r_hi, start=False, stop=False)
                            pe.matmul(o, l_hi, r_lo, start=False, stop=True).then_inc(misc_ready, 1)

                        def values(b, sh, half):
                            cols = slice(half * BANK, (half + 1) * BANK)
                            for j in range(QT):
                                unit = ("V", (b, sh), half * QT + j)
                                o = claim(unit)
                                tok = slice(j * P, (j + 1) * P)
                                split_product(o, xT_hi[:, tok], xT_lo[:, tok], W_hi[:, 2, cols], W_lo[:, 2, cols])

                        def project(b, sh, p):
                            cols = slice(p * P, (p + 1) * P)
                            if p == 0:
                                pe.wait_ge(misc_read_dve, misc.linear(lambda n: misc.read["dve"][n], ("T", (b, sh), 0)))
                            for name, w in (("Qm", 0), ("Qr", 3), ("Km", 1), ("Kr", 4)):
                                o = claim((name, (b, sh), p))
                                split_product(o, W_hi[:, w, cols], W_lo[:, w, cols], xT_hi[:, :], xT_lo[:, :])

                        def scores(b, h):
                            p = h // 2
                            if h % 2 == 0:
                                pe.wait_ge(qk_ready, pair_no(b, 0, p) + 1)
                            for u, tiles in enumerate(SCORE_UNITS):
                                for i in tiles:
                                    bank, at = SCORE_AT[i]
                                    pe.matmul(flat[:, at:at + (i + 1) * P], Qp[:, p % 2, h % 2, i * P:(i + 1) * P],
                                              Kp[:, p % 2, 0:(i + 1) * P], start=True, stop=False)
                                    mm = pe.matmul(flat[:, at + i * P:at + (i + 1) * P], ident_b[:, :], mask_b[:, :],
                                                   start=False, stop=True)
                                mm.then_inc(scores_ready, 1)

                        def turn_probs(b, sh, h, start=False):
                            k = head_no(b, sh, h)
                            pe.wait_ge(exp_done, k * 3 + 3)
                            for u, tiles in enumerate(PROBT_UNITS):
                                bank = PT_BANK + (3 * h + u) % 2
                                if u == 0 and not start:
                                    pe.wait_ge(pt_copied_act, k * 2)
                                if u == 1 and not start:
                                    pe.wait_ge(pt_copied_dve, k)
                                if u == 2:
                                    pe.wait_ge(pt_copied_act, k * 2 + 1)
                                col = 0
                                for j in tiles:
                                    for i in range(j, QT):
                                        at = SCORE_AT[i][1] + j * P
                                        mm = pe.transpose(banks[:, bank, col:col + P], probs[:, at:at + P], ident[:, :])
                                        col += P
                                mm.then_inc(pt_ready, 1)

                        def weigh_values(b, sh, p, start=False):
                            k = pair_no(b, sh, p)
                            pe.wait_ge(pt_copied_act, k * 4 + 4)
                            pe.wait_ge(pt_copied_dve, k * 2 + 2)
                            if p in (0, NPAIR // 2):
                                pe.wait_ge(misc_read_act, misc.linear(
                                    lambda n: misc.read["act"][n], ("V", (b, sh), QT - 1 if p == 0 else 2 * QT - 1)))
                            if not start:
                                pe.wait_ge(o_ready, k)
                            for j in range(QT):
                                at = PROBT_AT[j][1]
                                for a in range(2):
                                    hd = 2 * p + a
                                    mm = pe.matmul(banks[a * DK:(a + 1) * DK, O_BANK, j * P:S],
                                                   V[:, j, hd * DK:(hd + 1) * DK],
                                                   probsT[:, a, at:at + S - j * P], start=(j == 0), stop=(j == QT - 1))
                            mm.then_inc(pv_ready, 1)

                        def spread_den(b, sh, p):
                            o = claim(("R", (b, sh), p))
                            pe.wait_ge(inv_ready, pair_no(b, sh, p) + 1)
                            for i in range(QT):
                                mm = pe.transpose(o[:, i * P:(i + 1) * P], inv_wide[:, i, :], ident[:, :])
                            mm.then_inc(misc_ready, 1)

                        def out_project(b, sh):
                            o = claim(("O", (b, sh), 0))
                            pe.wait_ge(o_ready, pair_no(b, sh, NPAIR - 1) + 1)
                            for i in range(QT):
                                for p in range(NPAIR):
                                    mm = pe.matmul(o[:, i * P:(i + 1) * P], OT[:, p, i * P:(i + 1) * P], WoT[:, p, :],
                                                   start=(p == 0), stop=(p == NPAIR - 1))
                            mm.then_inc(misc_ready, 1)

                        def prologue():
                            pe.wait_ge(padded, 1)
                            turn(0, 0)
                            pe.wait_ge(misc_read_dve, misc.linear(lambda n: misc.read["dve"][n], ("T", (0, 0), 0)))
                            values(0, 0, 0)
                            project(0, 0, 0)
                            project(0, 0, 1)

                        def body(b, first, last):
                            for p in range(NPAIR):
                                sh, pp = before(b, p, 1)
                                started = not (first and p == 0)
                                if started:
                                    turn_probs(b, sh, 2 * pp + 1)
                                scores(b, 2 * p)
                                if started:
                                    weigh_values(b, sh, pp, first and p == 1)
                                    spread_den(b, sh, pp)
                                turn_probs(b, 0, 2 * p, first and p == 0)
                                scores(b, 2 * p + 1)
                                nsh, np_ = after(p, 2)
                                if not (last and nsh):
                                    project(b, nsh, np_)
                                if p == 0:
                                    values(b, 0, 1)
                                    if not first:
                                        out_project(b, -1)
                                if p == 5 and not last:
                                    turn(b, 1)
                                if p == 7 and not last:
                                    values(b, 1, 0)

                        def epilogue():
                            turn_probs(B - 1, 0, H - 1)
                            weigh_values(B - 1, 0, NPAIR - 1)
                            spread_den(B - 1, 0, NPAIR - 1)
                            out_project(B - 1, 0)

                        batches(pe, prologue, body, epilogue)

                    @block.scalar
                    def _(act):
                        def bank_of(unit):
                            act.wait_ge(misc_ready, misc.ready(unit))
                            return banks[:, MISC_BANK + misc.bank(unit), :]

                        def high(b, sh):
                            o = bank_of(("T", (b, sh), 0))
                            act.activation(xT_hi[:, :], o, ACT.Copy).then_inc(T_hi, 1)

                        def values(b, sh, half, start=False):
                            for j in range(QT):
                                o = bank_of(("V", (b, sh), half * QT + j))
                                if j == 0 and not start:
                                    act.wait_ge(pv_ready, pair_no(b, sh - 1, (NPAIR // 2) * (half + 1) - 1) + 1)
                                act.activation(V[:, j, half * BANK:(half + 1) * BANK], o, ACT.Copy).then_inc(misc_read_act, 1)

                        def exps(b, h):
                            k = head_no(b, 0, h)
                            p = h // 2
                            for u, tiles in enumerate(SCORE_UNITS):
                                act.wait_ge(max_ready, k * 3 + u + 1)
                                for i in tiles:
                                    at = SCORE_AT[i][1]
                                    cols = slice(at, at + (i + 1) * P)
                                    ex = act.activation(probs[:, cols], flat[:, cols], ACT.Exp,
                                                        bias=negmax[:, h % 2, i:i + 1],
                                                        accum_out=den[:, p % 2, i, h % 2:h % 2 + 1])
                                ex.then_inc(exp_done, 1)

                        def copy_pt(b, sh, h):
                            k = head_no(b, sh, h)
                            for u in range(2):
                                act.wait_ge(pt_ready, k * 3 + u + 1)
                                act.activation(probsT[:, h % 2, u * BANK:(u + 1) * BANK],
                                               banks[:, PT_BANK + (3 * h + u) % 2, :], ACT.Copy).then_inc(pt_copied_act, 1)

                        def copy_r(b, sh, p, start=False):
                            o = bank_of(("R", (b, sh), p))
                            if not start:
                                act.wait_ge(o_ready, pair_no(b, sh, p))
                            act.activation(R[:, :], o, ACT.Copy).then_inc(misc_read_act, 1)

                        def prologue():
                            high(0, 0)
                            values(0, 0, 0, True)

                        def body(b, first, last):
                            for p in range(NPAIR):
                                sh, pp = before(b, p, 1)
                                started = not (first and p == 0)
                                if started:
                                    copy_pt(b, sh, 2 * pp + 1)
                                exps(b, 2 * p)
                                if started:
                                    copy_r(b, sh, pp, first and p == 1)
                                copy_pt(b, 0, 2 * p)
                                exps(b, 2 * p + 1)
                                if p == 0:
                                    values(b, 0, 1, first)
                                if p == 5 and not last:
                                    high(b, 1)
                                if p == 7 and not last:
                                    values(b, 1, 0)

                        def epilogue():
                            copy_pt(B - 1, 0, H - 1)
                            copy_r(B - 1, 0, NPAIR - 1)

                        batches(act, prologue, body, epilogue)

                    @block.vector
                    def _(dve):
                        def bank_of(unit):
                            dve.wait_ge(misc_ready, misc.ready(unit))
                            return banks[:, MISC_BANK + misc.bank(unit), :]

                        def low(b, sh):
                            o = bank_of(("T", (b, sh), 0))
                            dve.wait_ge(T_hi, b + sh + 1)
                            dve.tensor_tensor(xT_lo[:, :], o, xT_hi[:, :].bitcast(F32), ALU.subtract).then_inc(misc_read_dve, 1)

                        def rotate(b, sh, p, start=False):
                            for n, name in enumerate(("Qm", "Qr", "Km", "Kr")):
                                o = bank_of((name, (b, sh), p))
                                if n == 0 and not start:
                                    dve.wait_ge(qk_ready, pair_no(b, sh, p))
                                dve.tensor_tensor(rot[:, n, :], o, tables[:, n, :], ALU.mult).then_inc(misc_read_dve, 1)

                        def maxima(b, h):
                            k = head_no(b, 0, h)
                            for u, tiles in enumerate(SCORE_UNITS):
                                dve.wait_ge(scores_ready, k * 3 + u + 1)
                                for i in tiles:
                                    at = SCORE_AT[i][1]
                                    mx = dve.tensor_reduce(negmax[:, h % 2, i:i + 1], flat[:, at:at + (i + 1) * P],
                                                           AX.X, ALU.max, negate=True)
                                mx.then_inc(max_ready, 1)

                        def copy_pt(b, sh, h):
                            k = head_no(b, sh, h)
                            dve.wait_ge(pt_ready, k * 3 + 3)
                            dve.tensor_copy(probsT[:, h % 2, 2 * BANK:PROB_COLS],
                                            banks[:, PT_BANK + (3 * h + 2) % 2, 0:PROB_COLS - 2 * BANK]
                                            ).then_inc(pt_copied_dve, 1)

                        def invert(b, sh, p):
                            dve.wait_ge(exp_done, pair_no(b, sh, p) * 6 + 6)
                            dve.reciprocal(inv_den[:, :, :], den[:, p % 2, :, :]).then_inc(inv_done, 1)
                            dve.wait_ge(inv_done, pair_no(b, sh, p) + 1)
                            dve.tensor_copy(inv_wide[:, :, :].rearrange("p i (a d) -> p i a d", a=2),
                                            inv_den[:, :, :].unsqueeze(3).broadcast_to([P, QT, 2, DK])
                                            ).then_inc(inv_ready, 1)

                        def normalise(b, sh, p, start=False):
                            dve.wait_ge(pv_ready, pair_no(b, sh, p) + 1)
                            dve.wait_ge(misc_read_act, misc.linear(lambda n: misc.read["act"][n], ("R", (b, sh), p)))
                            if p == 0 and not start:
                                dve.wait_ge(misc_ready, misc.ready(("O", (b, sh - 1), 0)))
                            dve.tensor_tensor(OT[:, p, :], banks[:, O_BANK, :], R[:, :], ALU.mult).then_inc(o_ready, 1)

                        def add_residual(b, sh):
                            o = bank_of(("O", (b, sh), 0))
                            xb = X[:, bass.ds((b + sh) * QT, QT), :]
                            dve.tensor_tensor(xb, o.rearrange("p (t d) -> p t d", t=QT), xb, ALU.add).then_inc(misc_read_dve, 1)

                        def prologue():
                            dve.memset(Qp[:, :, :, :], 0.0).then_inc(padded, 1)
                            norm_stats(dve, 0, "attn")
                            norm_apply(dve, 0, "attn")
                            low(0, 0)
                            rotate(0, 0, 0, True)
                            rotate(0, 0, 1)

                        def body(b, first, last):
                            for p in range(NPAIR):
                                sh, pp = before(b, p, 1)
                                started = not (first and p == 0)
                                if started:
                                    invert(b, sh, pp)
                                    copy_pt(b, sh, 2 * pp + 1)
                                maxima(b, 2 * p)
                                if started:
                                    normalise(b, sh, pp, first)
                                copy_pt(b, 0, 2 * p)
                                maxima(b, 2 * p + 1)
                                nsh, np_ = after(p, 2)
                                if not (last and nsh):
                                    rotate(b, nsh, np_)
                                if p == 0 and not first:
                                    add_residual(b, -1)
                                if p == 2 and not last:
                                    norm_stats(dve, b + 1, "attn")
                                if p == 3 and not last:
                                    norm_apply(dve, b + 1, "attn")
                                if p == 5 and not last:
                                    low(b, 1)

                        def epilogue():
                            invert(B - 1, 0, NPAIR - 1)
                            copy_pt(B - 1, 0, H - 1)
                            normalise(B - 1, 0, NPAIR - 1)
                            add_residual(B - 1, 0)

                        batches(dve, prologue, body, epilogue)

                    @block.gpsimd
                    def _(pool):
                        def add_up(b, sh, p, start=False):
                            r = p % 2
                            k = pair_no(b, sh, p)
                            if not start:
                                pool.wait_ge(scores_ready, k * 6 - 6)
                            pool.wait_ge(misc_read_dve, misc.linear(lambda n: misc.read["dve"][n], ("Kr", (b, sh), p)))
                            pool.tensor_tensor(Qp[0:DK, r, 0, :], rot[0:DK, 0, :], rot[0:DK, 1, :],
                                               ALU.add).then_inc(half_added, 1)
                            pool.wait_ge(half_added, 2 * k + 1)
                            pool.tensor_tensor(Qp[DK:P, r, 1, :], rot[DK:P, 0, :], rot[DK:P, 1, :],
                                               ALU.add).then_inc(half_added, 1)
                            pool.wait_ge(half_added, 2 * k + 2)
                            pool.tensor_tensor(Kp[:, r, :], rot[:, 2, :], rot[:, 3, :], ALU.add).then_inc(qk_ready, 1)

                        def prologue():
                            norm_rstd(pool, 0, "attn")
                            pool.wait_ge(padded, 1)
                            add_up(0, 0, 0, True)
                            add_up(0, 0, 1, True)

                        def body(b, first, last):
                            for p in range(NPAIR):
                                nsh, np_ = after(p, 2)
                                if not (last and nsh):
                                    add_up(b, nsh, np_)
                                if p == 2 and not last:
                                    norm_rstd(pool, b + 1, "attn")

                        batches(pool, prologue, body, lambda: None)

        ffn("ffn1", False)
        attention()
        ffn("ffn2", True)


def shape_tables():
    inv_freq = (1.0 / np.power(np.float32(6000.0), np.arange(0, ROPE, 2, dtype=np.float32) / np.float32(ROPE))).astype(np.float32)
    angle = np.outer(np.arange(S, dtype=np.float32), inv_freq).astype(np.float32)
    cos, sin = np.cos(angle).astype(np.float32).T, np.sin(angle).astype(np.float32).T
    c = np.ones((DK, S), np.float32)
    s = np.zeros((DK, S), np.float32)
    c[0:16], c[16:32] = cos, cos
    s[0:16], s[16:32] = -sin, sin
    c, s = np.concatenate([c, c]), np.concatenate([s, s])
    scale = np.float32(1.0 / np.sqrt(DK))
    e = np.arange(E)
    rank = np.stack([e[None, :] > e[:, None], e[None, :] < e[:, None]]).astype(np.float32)
    mask = np.where(np.arange(P)[None, :] > np.arange(P)[:, None], np.float32(-1e30), np.float32(0))
    return {
        "cos_q": c * scale, "sin_q": s * scale, "cos_k": c, "sin_k": s, "ident": np.eye(P, dtype=np.float32),
        "rank": np.ascontiguousarray(np.broadcast_to(rank, (P, 2, E, E))), "mask": mask.astype(np.float32),
    }


_INS = ['L0_attn_x', 'L0_attn_W_qkv', 'L0_attn_W_o', 'L0_ffn_Wr', 'L0_ffn_Wi', 'L0_ffn_Wo']


def kernel(**inputs):
    import concourse.bacc as _bacc
    from concourse.bass_utils import run_bass_kernel_spmd as _run

    nc = _bacc.Bacc("TRN2", target_bir_lowering=False, num_devices=1)
    arrays, args = {}, []
    for name, a in [(n, inputs[n]) for n in _INS] + list(shape_tables().items()):
        a = np.ascontiguousarray(a)
        arrays[f"in_{name}_dram"] = a
        args.append(nc.dram_tensor(f"in_{name}_dram", a.shape, mybir.dt.from_np(a.dtype), kind="ExternalInput").ap())
    args.append(nc.dram_tensor("out_dram", (B, S, D), F32, kind="ExternalOutput").ap())
    build(nc, *args)
    r = _run(nc, [arrays], core_ids=[0])
    return r.results[0]["out_dram"]
```

```python
import concourse.bass as bass
from concourse import mybir
from contextlib import ExitStack
import numpy as np

F32 = mybir.dt.float32
F32R = mybir.dt.float32r
BF16 = mybir.dt.bfloat16
ALU = mybir.AluOpType
ACT = mybir.ActivationFunctionType
AX = mybir.AxisListType

P = 128
B, S, D = 16, 512, 128
H, DK = 16, 64
E = 8
TOPK = 2
EPS = 1e-5
ROPE = DK // 2
QT = S // P
NPAIR = H // 2
BANK = 512

SCORE_AT = {3: (0, 0), 2: (1, 512), 0: (1, 896), 1: (2, 1024)}
SCORE_UNITS = [[3], [2, 0], [1]]
PROBT_AT = {2: (0, 0), 0: (1, 256), 1: (2, 768), 3: (2, 1152)}
PROBT_UNITS = [[2], [0], [1, 3]]
PROBT_WIDTH = [256, 512, 512]
PROB_COLS = 1280


EXTRAS = {
    (0, "mid"): [("V", 0, 4), ("V", 0, 5)],
    (0, "end"): [("O", -1, 0)],
    (0, "late"): [("T1", 1, 0)],
    (1, "mid"): [("V", 0, 6), ("V", 0, 7)],
    (1, "end"): [("LT1", 1, 0)],
    (1, "late"): [("T2", -1, 0)],
    (2, "mid"): [("L1", 1, 0)],
    (2, "end"): [("LT2", -1, 0), ("Y1", 1, 0), ("Y1", 1, 1)],
    (3, "mid"): [("Y1", 1, 2), ("Y1", 1, 3)],
    (3, "end"): [("Y1", 1, 4)],
    (4, "mid"): [("Y1", 1, 5), ("Y1", 1, 6)],
    (4, "end"): [("Y1", 1, 7)],
    (5, "mid"): [("L2", -1, 0)],
    (5, "end"): [("Y2", -1, 0), ("Y2", -1, 1)],
    (5, "late"): [("T", 1, 0)],
    (6, "mid"): [("V", 1, 0), ("V", 1, 1)],
    (6, "end"): [("Y2", -1, 2), ("Y2", -1, 3), ("Y2", -1, 4)],
    (7, "mid"): [("V", 1, 2), ("V", 1, 3)],
    (7, "end"): [("Y2", -1, 5), ("Y2", -1, 6), ("Y2", -1, 7)],
}
PROLOGUE = ([("T1", 0, 0), ("LT1", 0, 0), ("L1", 0, 0)] + [("Y1", 0, i) for i in range(2 * QT)] + [("T", 0, 0)]
            + [("V", 0, j) for j in range(QT)])
EPILOGUE = [("O", 0, 0), ("T2", 0, 0), ("LT2", 0, 0), ("L2", 0, 0)] + [("Y2", 0, i) for i in range(2 * QT)]


def extras(p, slot, first, last):
    return [u for u in EXTRAS.get((p, slot), ()) if not (first and u[1] < 0) and not (last and u[1] > 0)]


def before(p):
    return (0, p - 1) if p else (-1, NPAIR - 1)


def after(p, ahead):
    return (0, p + ahead) if p + ahead < NPAIR else (1, p + ahead - NPAIR)


def whole_order():
    order = [(k, b, i) for k, b, i in PROLOGUE] + [(k, 0, p) for p in (0, 1) for k in ("Q", "K")]
    for b in range(B):
        for p in range(NPAIR):
            order += [(k, b + sh, i) for k, sh, i in extras(p, "mid", b == 0, b == B - 1)]
            sh, pp = before(p)
            if b + sh >= 0:
                order.append(("R", b + sh, pp))
            order += [(k, b + sh, i) for k, sh, i in extras(p, "end", b == 0, b == B - 1)]
            sh, pn = after(p, 2)
            if b + sh < B:
                order += [("Q", b + sh, pn), ("K", b + sh, pn)]
            order += [(k, b + sh, i) for k, sh, i in extras(p, "late", b == 0, b == B - 1)]
    return order + [("R", B - 1, NPAIR - 1)] + [(k, B - 1, i) for k, _, i in EPILOGUE]


class Counts:

    MID = 5

    def __init__(self, events):
        self.at = {e: n + 1 for n, e in enumerate(events)}

    def __call__(self, kind, b, shift, index=0, less=0):
        if isinstance(b, int):
            return self.at[(kind, b + shift, index)] - less
        one, two = (self.at[(kind, m + shift, index)] for m in (self.MID, self.MID + 1))
        return b * (two - one) + (one - less - self.MID * (two - one))


READER = {"V": "act", "R": "act", "LT1": "act", "LT2": "act", "L1": "act", "L2": "act"}


class Banks:

    def __init__(self, units):
        self.units = units
        self.ready = Counts(units)
        self.read = {who: Counts([u for u in units if READER.get(u[0], "dve") == who]) for who in ("act", "dve")}

    def place(self, kind, b, shift, index=0):
        return self.ready.at[(kind, (b if isinstance(b, int) else Counts.MID) + shift, index)] - 1

    def bank(self, *unit):
        return self.place(*unit) % 2

    def reader(self, kind):
        return READER.get(kind, "dve")

    def free(self, kind, b, shift, index=0):
        n = self.place(kind, b, shift, index)
        if n < 2:
            return None
        k, bb, i = self.units[n - 2]
        who = self.reader(k)
        if isinstance(b, int):
            return who, self.read[who](k, bb, 0, i)
        return who, self.read[who](k, b, bb - Counts.MID, i)


def build(nc, x, w_qkv, w_o, w_r, w_i, w_out, cos_q, sin_q, cos_k, sin_k, ident_d, rank_d, mask_d, out):
    outer = ExitStack()
    with outer:
        def sb(name, shape, dt=F32, stack=outer):
            return stack.enter_context(nc.sbuf_tensor(name, shape, dt))

        def sem(name, stack=outer):
            return stack.enter_context(nc.semaphore(name))

        X = sb("X", [P, B * QT, D])
        W_hi = sb("W_hi", [P, 3, H * DK], F32R)
        W_lo = sb("W_lo", [P, 3, H * DK], F32R)
        WoT = sb("WoT", [P, NPAIR, D])
        M_hi = sb("M_hi", [P, E * D], F32R)
        M_lo = sb("M_lo", [P, E * D], F32R)
        Wr_hi = sb("Wr_hi", [P, P], F32R)
        Wr_lo = sb("Wr_lo", [P, P], F32R)
        tables = sb("tables", [P, 4, S])
        ident = sb("ident", [P, P])
        ident_b = sb("ident_b", [P, P], BF16)
        mask_b = sb("mask_b", [P, P], BF16)
        ranks = sb("ranks", [P, 2, E, E])
        minus_half = sb("minus_half", [P, QT])
        banks = outer.enter_context(nc.psum_tensor("banks", [P, 8, BANK], F32))
        flat = banks[:, :, :].rearrange("p a b -> p (a b)")

        with ExitStack() as st:
            wn = sb("wn", [P, 24, P], stack=st)
            won = sb("won", [P, H * DK], stack=st)
            win = sb("win", [P, E, P], stack=st)
            wit = sb("wit", [P, E, P], stack=st)
            woutn = sb("woutn", [P, E, P], stack=st)
            wrn = sb("wrn", [P, P], stack=st)
            mask_f = sb("mask_f", [P, P], stack=st)
            x_in, const_in, w_in, wo_in, wi_in, wout_in = (sem(n, st) for n in (
                "x_in", "const_in", "w_in", "wo_in", "wi_in", "wout_in"))
            turned, hi_done, lo_done, cast, prod_ready, filled = (sem(n, st) for n in (
                "turned", "hi_done", "lo_done", "cast", "prod_ready", "filled"))
            NW = 6
            with nc.Block() as block:

                @block.sync
                def _(sp):
                    sp.dma_start(ident[:, :], ident_d).then_inc(const_in, 16)
                    sp.dma_start(wn[:, :, :], w_qkv.rearrange("q h d m -> (q h d) m").rearrange(
                        "(t p) m -> p t m", p=P)).then_inc(w_in, 16)
                    sp.dma_start(won[:, :], w_o).then_inc(wo_in, 16)
                    sp.dma_start(X[:, 0:32, :], x.rearrange("b (t p) d -> p (b t) d", p=P)[:, 0:32, :]).then_inc(x_in, 16)
                    sp.wait_ge(x_in, 32)

                @block.scalar
                def _(act):
                    act.dma_start(win[:, :, :], w_i.rearrange("e d h -> d e h")).then_inc(wi_in, 16)
                    act.dma_start(woutn[:, :, :], w_out.rearrange("e h d -> h e d")).then_inc(wout_in, 16)
                    act.wait_ge(filled, 1)
                    act.dma_start(wrn[:, 0:E], w_r).then_inc(const_in, 16)
                    act.dma_start(mask_f[:, :], mask_d).then_inc(const_in, 16)
                    act.dma_start(ranks[:, :, :, :], rank_d).then_inc(const_in, 16)
                    for n, t in enumerate((cos_q, sin_q, cos_k, sin_k)):
                        act.dma_start(tables[:, n, :], t).then_inc(const_in, 16)
                    act.dma_start(X[:, 32:64, :], x.rearrange("b (t p) d -> p (b t) d", p=P)[:, 32:64, :]).then_inc(x_in, 16)
                    for g in range(NW):
                        act.wait_ge(turned, g + 1)
                        act.activation(W_hi[:, g // 2, (g % 2) * BANK:(g % 2 + 1) * BANK], banks[:, g, :],
                                       ACT.Copy).then_inc(hi_done, 1)
                    for g in range(2):
                        act.wait_ge(turned, NW + g + 1)
                        act.activation(WoT[:, 4 * g:4 * g + 4, :], banks[:, 6 + g, :].rearrange("p (a b) -> p a b", a=4),
                                       ACT.Copy).then_inc(hi_done, 1)
                    for g in range(2):
                        act.wait_ge(turned, NW + 2 + g + 1)
                        act.activation(wit[:, 4 * g:4 * g + 4, :], banks[:, g, :].rearrange("p (a b) -> p a b", a=4),
                                       ACT.Copy).then_inc(hi_done, 1)
                    for g in range(2):
                        act.wait_ge(prod_ready, g + 1)
                        act.activation(M_hi[:, g * BANK:(g + 1) * BANK], banks[:, 2 + g, :], ACT.Copy).then_inc(hi_done, 1)
                    act.wait_ge(const_in, 16 * 8)
                    act.activation(Wr_hi[:, :], wrn[:, :], ACT.Copy).then_inc(hi_done, 1)

                @block.tensor
                def _(pe):
                    pe.wait_ge(const_in, 16 * 8)
                    pe.wait_ge(w_in, 16)
                    for g in range(NW):
                        for a in range(4):
                            mm = pe.transpose(banks[:, g, a * P:(a + 1) * P], wn[:, 4 * g + a, :], ident[:, :])
                        mm.then_inc(turned, 1)
                    pe.wait_ge(wo_in, 16)
                    for g in range(2):
                        for a in range(4):
                            mm = pe.transpose(banks[:, 6 + g, a * P:(a + 1) * P],
                                              won[:, (4 * g + a) * P:(4 * g + a + 1) * P], ident[:, :])
                        mm.then_inc(turned, 1)
                    pe.wait_ge(wi_in, 16)
                    for g in range(2):
                        pe.wait_ge(lo_done, g + 1)
                        for a in range(4):
                            mm = pe.transpose(banks[:, g, a * P:(a + 1) * P], win[:, 4 * g + a, :], ident[:, :])
                        mm.then_inc(turned, 1)
                    pe.wait_ge(wout_in, 16)
                    pe.wait_ge(hi_done, NW + 4)
                    pe.wait_ge(lo_done, 4)
                    for g in range(2):
                        for a in range(4):
                            e = 4 * g + a
                            mm = pe.matmul(banks[:, 2 + g, a * P:(a + 1) * P], wit[:, e, :], woutn[:, e, :],
                                           start=True, stop=True)
                        mm.then_inc(prod_ready, 1)

                @block.vector
                def _(dve):
                    dve.memset(minus_half[:, :], -0.5)
                    dve.memset(wrn[:, :], 0.0).then_inc(filled, 1)
                    for g in range(NW):
                        dve.wait_ge(hi_done, g + 1)
                        cols = slice((g % 2) * BANK, (g % 2 + 1) * BANK)
                        dve.tensor_tensor(W_lo[:, g // 2, cols], banks[:, g, :], W_hi[:, g // 2, cols].bitcast(F32),
                                          ALU.subtract).then_inc(lo_done, 1)
                    for g in range(2):
                        dve.wait_ge(hi_done, NW + 4 + g + 1)
                        cols = slice(g * BANK, (g + 1) * BANK)
                        dve.tensor_tensor(M_lo[:, cols], banks[:, 2 + g, :], M_hi[:, cols].bitcast(F32),
                                          ALU.subtract).then_inc(lo_done, 1)
                    dve.wait_ge(hi_done, NW + 7)
                    dve.tensor_tensor(Wr_lo[:, :], wrn[:, :], Wr_hi[:, :].bitcast(F32), ALU.subtract).then_inc(lo_done, 1)
                    dve.wait_ge(const_in, 16 * 8)
                    dve.tensor_copy(ident_b[:, :], ident[:, :]).then_inc(cast, 1)
                    dve.tensor_copy(mask_b[:, :], mask_f[:, :]).then_inc(cast, 1)
                    dve.wait_ge(cast, 2)

        with ExitStack() as st:
            def asb(name, shape, dt=F32):
                return sb(name, shape, dt, st)

            def asem(name):
                return sem(name, st)

            order = whole_order()
            shared = Banks(order)
            norms = Counts([u for u in order if u[0] in ("T", "T1", "T2")])
            routes = Counts([u for u in order if u[0] in ("L1", "L2")])
            tiles = Counts([(k, b, i // 2) for k, b, i in order if k in ("Y1", "Y2") and i % 2])

            stats = asb("stats", [P, QT, 6])
            meanvar = asb("meanvar", [P, QT, 2])
            var_eps = asb("var_eps", [P, QT])
            rstd = asb("rstd", [P, QT])
            carrier = asb("carrier", [P, 1])
            xn = asb("xn", [P, QT, D])
            xT_hi = {w: asb(f"xT{w}_hi", [P, S], F32R) for w in ("", "1", "2")}
            xT_lo = {w: asb(f"xT{w}_lo", [P, S], F32R) for w in ("", "1", "2")}
            logitT = asb("logitT", [P, S])
            logit = asb("logit", [P, QT, E])
            top = asb("top", [P, QT])
            shifted = asb("shifted", [P, QT, E])
            expo = asb("expo", [P, QT, E])
            total = asb("total", [P, QT])
            inv_total = asb("inv_total", [P, QT])
            gt = asb("gt", [P, QT, E, E])
            ge = asb("ge", [P, QT, E, E])
            rank = asb("rank", [P, QT, E])
            taken = asb("taken", [P, QT, E])
            chosen = asb("chosen", [P, QT, E])
            gate = {w: asb(f"gate{w}", [P, QT, E]) for w in ("1", "2")}
            Z = asb("Z", [P, 2, E, D])
            V = asb("V", [P, QT, H * DK])
            rot = asb("rot", [P, 2, 4, S])
            Q_hi = asb("Q_hi", [P, 2, 2, S], F32R)
            Q_lo = asb("Q_lo", [P, 2, 2, S], F32R)
            K_hi = asb("K_hi", [P, 2, S], F32R)
            K_lo = asb("K_lo", [P, 2, S], F32R)
            probs = asb("probs", [P, PROB_COLS])
            probsT = asb("probsT", [P, 2, PROB_COLS])
            negmax = asb("negmax", [P, 2, QT])
            den = asb("den", [P, 2, QT, 2])
            inv_den = asb("inv_den", [P, QT, 2])
            inv_wide = asb("inv_wide", [P, QT, P])
            R = asb("R", [P, S])
            OT = asb("OT", [P, NPAIR, S])

            shared_ready, shared_read_act, shared_read_dve = (
                asem(n) for n in ("shared_ready", "shared_read_act", "shared_read_dve"))
            stats_done, agg_done, eps_done, rstd_done, xn_done, high_done = (
                asem(n) for n in ("stats_done", "agg_done", "eps_done", "rstd_done", "xn_done", "high_done"))
            g_top, g_cmp, g_mul, g_add, g_rank, g_take, g_tot, g_inv, g_pick = (
                asem(n) for n in ("g_top", "g_cmp", "g_mul", "g_add", "g_rank", "g_take", "g_tot", "g_inv", "g_pick"))
            shift_done, expo_done, gate_done, z_done, z_adds, summed, out_done = (
                asem(n) for n in ("shift_done", "expo_done", "gate_done", "z_done", "z_adds", "summed", "out_done"))
            padded, rotated, turned_half, qk_sum, qk_high, q_low, qk_done = (
                asem(n) for n in ("padded", "rotated", "turned_half", "qk_sum", "qk_high", "q_low", "qk_done"))
            scores_ready, max_done, exp_done, pt_ready, pt_copied = (
                asem(n) for n in ("scores_ready", "max_done", "exp_done", "pt_ready", "pt_copied"))
            pv_ready, inv_done, wide_done, o_done = (
                asem(n) for n in ("pv_ready", "inv_done", "wide_done", "o_done"))
            SHARED_BANK, O_BANK = 3, 7
            PROBT_COL = [3 * BANK - PROBT_WIDTH[0], 5 * BANK, 6 * BANK]

            def head_no(b, shift, h):
                return (b + shift) * H + h

            def pair_no(b, shift, p):
                return (b + shift) * NPAIR + p

            def batches(engine, prologue, body, epilogue):
                prologue()
                body(0, True, False)
                with engine.Fori(1, B - 1) as b:
                    body(b, False, False)
                body(B - 1, False, True)
                epilogue()

            with nc.Block() as block:

                @block.tensor
                def _(pe):
                    def claim(*unit):
                        free = shared.free(*unit)
                        if free:
                            pe.wait_ge(shared_read_act if free[0] == "act" else shared_read_dve, free[1])
                        return banks[:, SHARED_BANK + shared.bank(*unit), :]

                    def split_product(o, l_hi, l_lo, r_hi, r_lo):
                        pe.matmul(o, l_hi, r_hi, start=True, stop=False)
                        pe.matmul(o, l_hi, r_lo, start=False, stop=False)
                        return pe.matmul(o, l_lo, r_hi, start=False, stop=True)

                    def both_parts(w, b, sh):
                        pe.wait_ge(shared_read_dve, shared.read["dve"]("T" + w, b, sh))

                    def turn(w, b, sh):
                        o = claim("T" + w, b, sh)
                        pe.wait_ge(xn_done, norms("T" + w, b, sh))
                        for i in range(QT):
                            mm = pe.transpose(o[:, i * P:(i + 1) * P], xn[:, i, :], ident[:, :])
                        mm.then_inc(shared_ready, 1)

                    def logits_T(w, b, sh):
                        o = claim("LT" + w, b, sh)
                        both_parts(w, b, sh)
                        split_product(o, Wr_hi[:, :], Wr_lo[:, :], xT_hi[w][:, :], xT_lo[w][:, :]).then_inc(shared_ready, 1)

                    def logits(w, b, sh):
                        o = claim("L" + w, b, sh)
                        pe.wait_ge(shared_read_act, shared.read["act"]("LT" + w, b, sh))
                        for i in range(QT):
                            mm = pe.transpose(o[:, i * P:(i + 1) * P], logitT[:, i * P:(i + 1) * P], ident[:, :])
                        mm.then_inc(shared_ready, 1)

                    def experts(w, b, sh, i):
                        o = claim("Y" + w, b, sh, i)
                        tok, cols = slice(i // 2 * P, (i // 2 + 1) * P), slice(i % 2 * BANK, (i % 2 + 1) * BANK)
                        split_product(o, xT_hi[w][:, tok], xT_lo[w][:, tok], M_hi[:, cols], M_lo[:, cols]
                                      ).then_inc(shared_ready, 1)

                    def values(b, sh, i):
                        o = claim("V", b, sh, i)
                        half, j = i // QT, i % QT
                        cols, tok = slice(half * BANK, (half + 1) * BANK), slice(j * P, (j + 1) * P)
                        both_parts("", b, sh)
                        split_product(o, xT_hi[""][:, tok], xT_lo[""][:, tok], W_hi[:, 2, cols], W_lo[:, 2, cols]
                                      ).then_inc(shared_ready, 1)

                    def project(b, sh, p):
                        cols = slice(p * P, (p + 1) * P)
                        both_parts("", b, sh)
                        for name, w in (("Q", 0), ("K", 1)):
                            o = claim(name, b, sh, p)
                            split_product(o, W_hi[:, w, cols], W_lo[:, w, cols], xT_hi[""][:, :], xT_lo[""][:, :]
                                          ).then_inc(shared_ready, 1)

                    def scores(b, h, start=False):
                        r, a = (h // 2) % 2, h % 2
                        if a == 0:
                            pe.wait_ge(qk_done, pair_no(b, 0, h // 2) + 1)
                        for u, tiles_ in enumerate(SCORE_UNITS):
                            if u == 2 and not start:
                                pe.wait_ge(pt_copied, head_no(b, 0, h) * 3 - 2)
                            for i in tiles_:
                                at, n, q = SCORE_AT[i][1], (i + 1) * P, slice(i * P, (i + 1) * P)
                                pe.matmul(flat[:, at:at + n], Q_hi[:, r, a, q], K_hi[:, r, 0:n], start=True, stop=False)
                                pe.matmul(flat[:, at:at + n], Q_hi[:, r, a, q], K_lo[:, r, 0:n], start=False, stop=False)
                                pe.matmul(flat[:, at:at + n], Q_lo[:, r, a, q], K_hi[:, r, 0:n], start=False, stop=False)
                                mm = pe.matmul(flat[:, at + i * P:at + n], ident_b[:, :], mask_b[:, :],
                                               start=False, stop=True)
                            mm.then_inc(scores_ready, 1)

                    def turn_probs(b, sh, h, start=False):
                        k = head_no(b, sh, h)
                        pe.wait_ge(exp_done, k * 3 + 3)
                        for u, tiles_ in enumerate(PROBT_UNITS):
                            if not start:
                                pe.wait_ge(pt_copied, k * 3 + u - 2)
                            col = PROBT_COL[u]
                            for j in tiles_:
                                for i in range(j, QT):
                                    at = SCORE_AT[i][1] + j * P
                                    mm = pe.transpose(flat[:, col:col + P], probs[:, at:at + P], ident[:, :])
                                    col += P
                            mm.then_inc(pt_ready, 1)

                    def weigh_values(b, sh, p, start=False):
                        k = pair_no(b, sh, p)
                        pe.wait_ge(pt_copied, k * 6 + 6)
                        if p in (0, NPAIR // 2):
                            pe.wait_ge(shared_read_act, shared.read["act"]("V", b, sh, QT - 1 if p == 0 else 2 * QT - 1))
                        if not start:
                            pe.wait_ge(o_done, k)
                        for j in range(QT):
                            at = PROBT_AT[j][1]
                            for a in range(2):
                                hd = 2 * p + a
                                mm = pe.matmul(banks[a * DK:(a + 1) * DK, O_BANK, j * P:S],
                                               V[:, j, hd * DK:(hd + 1) * DK],
                                               probsT[:, a, at:at + S - j * P], start=(j == 0), stop=(j == QT - 1))
                        mm.then_inc(pv_ready, 1)

                    def spread_den(b, sh, p):
                        o = claim("R", b, sh, p)
                        pe.wait_ge(wide_done, pair_no(b, sh, p) + 1)
                        for i in range(QT):
                            mm = pe.transpose(o[:, i * P:(i + 1) * P], inv_wide[:, i, :], ident[:, :])
                        mm.then_inc(shared_ready, 1)

                    def out_project(b, sh):
                        o = claim("O", b, sh)
                        pe.wait_ge(o_done, pair_no(b, sh, NPAIR - 1) + 1)
                        for i in range(QT):
                            for p in range(NPAIR):
                                mm = pe.matmul(o[:, i * P:(i + 1) * P], OT[:, p, i * P:(i + 1) * P], WoT[:, p, :],
                                               start=(p == 0), stop=(p == NPAIR - 1))
                        mm.then_inc(shared_ready, 1)

                    def run(units, b):
                        for kind, sh, i in units:
                            if kind[0] == "T":
                                turn(kind[1:], b, sh)
                            elif kind[:2] == "LT":
                                logits_T(kind[2:], b, sh)
                            elif kind[0] == "L":
                                logits(kind[1:], b, sh)
                            elif kind[0] == "Y":
                                experts(kind[1:], b, sh, i)
                            elif kind == "V":
                                values(b, sh, i)
                            elif kind == "O":
                                out_project(b, sh)

                    def prologue():
                        run(PROLOGUE, 0)
                        project(0, 0, 0)
                        project(0, 0, 1)
                        pe.wait_ge(padded, 2)

                    def body(b, first, last):
                        for p in range(NPAIR):
                            sh, pp = before(p)
                            started = not (first and p == 0)
                            if started:
                                turn_probs(b, sh, 2 * pp + 1, False)
                            scores(b, 2 * p, not started)
                            run(extras(p, "mid", first, last), b)
                            if started:
                                weigh_values(b, sh, pp, first and p == 1)
                                spread_den(b, sh, pp)
                            turn_probs(b, 0, 2 * p, not started)
                            scores(b, 2 * p + 1)
                            run(extras(p, "end", first, last), b)
                            nsh, pn = after(p, 2)
                            if not (last and nsh):
                                project(b, nsh, pn)
                            run(extras(p, "late", first, last), b)

                    def epilogue():
                        turn_probs(B - 1, 0, H - 1)
                        weigh_values(B - 1, 0, NPAIR - 1)
                        spread_den(B - 1, 0, NPAIR - 1)
                        run(EPILOGUE, B - 1)

                    batches(pe, prologue, body, epilogue)

                @block.scalar
                def _(act):
                    def bank_of(*unit):
                        act.wait_ge(shared_ready, shared.ready(*unit))
                        return banks[:, SHARED_BANK + shared.bank(*unit), :]

                    def high(w, b, sh):
                        act.activation(xT_hi[w][:, :], bank_of("T" + w, b, sh), ACT.Copy).then_inc(high_done, 1)

                    def copy_logits_T(w, b, sh):
                        act.activation(logitT[:, :], bank_of("LT" + w, b, sh), ACT.Copy).then_inc(shared_read_act, 1)

                    def routing(w, b, sh):
                        o = bank_of("L" + w, b, sh).rearrange("p (t n) -> p t n", n=P)[:, :, 0:E]
                        act.activation(logit[:, :, :], o, ACT.Copy).then_inc(shared_read_act, 1)
                        act.wait_ge(shift_done, routes("L" + w, b, sh))
                        act.activation(expo[:, :, :], shifted[:, :, :], ACT.Exp).then_inc(expo_done, 1)

                    def values(b, sh, i, start):
                        half, j = i // QT, i % QT
                        o = bank_of("V", b, sh, i)
                        if j == 0 and not start:
                            act.wait_ge(pv_ready, pair_no(b, sh - 1, (NPAIR // 2) * (half + 1) - 1) + 1)
                        act.activation(V[:, j, half * BANK:(half + 1) * BANK], o, ACT.Copy).then_inc(shared_read_act, 1)

                    def exps(b, h):
                        k, p = head_no(b, 0, h), h // 2
                        for u, tiles_ in enumerate(SCORE_UNITS):
                            act.wait_ge(max_done, k * 3 + u + 1)
                            for i in tiles_:
                                at = SCORE_AT[i][1]
                                cols = slice(at, at + (i + 1) * P)
                                ex = act.activation(probs[:, cols], flat[:, cols], ACT.Exp,
                                                    bias=negmax[:, h % 2, i:i + 1],
                                                    accum_out=den[:, p % 2, i, h % 2:h % 2 + 1])
                            ex.then_inc(exp_done, 1)

                    def copy_pt(b, sh, h):
                        k = head_no(b, sh, h)
                        for u in range(3):
                            n, at = PROBT_WIDTH[u], sum(PROBT_WIDTH[:u])
                            act.wait_ge(pt_ready, k * 3 + u + 1)
                            act.activation(probsT[:, h % 2, at:at + n],
                                           flat[:, PROBT_COL[u]:PROBT_COL[u] + n], ACT.Copy).then_inc(pt_copied, 1)

                    def copy_r(b, sh, p, start=False):
                        o = bank_of("R", b, sh, p)
                        if not start:
                            act.wait_ge(o_done, pair_no(b, sh, p))
                        act.activation(R[:, :], o, ACT.Copy).then_inc(shared_read_act, 1)

                    def high_qk(b, sh, p, start=False):
                        k, r = pair_no(b, sh, p), p % 2
                        if not start:
                            act.wait_ge(scores_ready, k * 6 - 6)
                        act.wait_ge(qk_sum, k * 2 + 2)
                        act.activation(K_hi[:, r, :], rot[:, r, 2, :], ACT.Copy).then_inc(qk_high, 1)
                        act.activation(Q_hi[0:DK, r, 0, :], rot[0:DK, r, 0, :], ACT.Copy)
                        act.activation(Q_hi[DK:P, r, 1, :], rot[DK:P, r, 0, :], ACT.Copy).then_inc(qk_high, 1)

                    def run(units, b, first=False):
                        for kind, sh, i in units:
                            if kind[0] == "T":
                                high(kind[1:], b, sh)
                            elif kind[:2] == "LT":
                                copy_logits_T(kind[2:], b, sh)
                            elif kind[0] == "L":
                                routing(kind[1:], b, sh)
                            elif kind == "V":
                                values(b, sh, i, first and sh == 0)

                    def prologue():
                        run(PROLOGUE, 0, True)
                        act.wait_ge(padded, 2)
                        high_qk(0, 0, 0, True)

                    def body(b, first, last):
                        for p in range(NPAIR):
                            sh, pp = before(p)
                            started = not (first and p == 0)
                            if started:
                                copy_pt(b, sh, 2 * pp + 1)
                            exps(b, 2 * p)
                            run(extras(p, "mid", first, last), b, first)
                            nsh, pn = after(p, 1)
                            if not (last and nsh):
                                high_qk(b, nsh, pn, not started)
                            if started:
                                copy_r(b, sh, pp, first and p == 1)
                            copy_pt(b, 0, 2 * p)
                            exps(b, 2 * p + 1)
                            run(extras(p, "end", first, last) + extras(p, "late", first, last), b, first)

                    def epilogue():
                        copy_pt(B - 1, 0, H - 1)
                        copy_r(B - 1, 0, NPAIR - 1)
                        run(EPILOGUE, B - 1)

                    batches(act, prologue, body, epilogue)

                @block.vector
                def _(dve):
                    def bank_of(*unit):
                        dve.wait_ge(shared_ready, shared.ready(*unit))
                        return banks[:, SHARED_BANK + shared.bank(*unit), :]

                    def norm_stats(w, b, sh):
                        k = norms("T" + w, b, sh)
                        if w == "":
                            dve.wait_ge(summed, tiles("Y1", b, sh, QT - 1))
                            dve.memset(carrier[:, :], 0.0)
                        if w == "2":
                            dve.wait_ge(shared_read_dve, shared.read["dve"]("O", b, sh))
                            dve.memset(carrier[:, :], 0.0)
                        for i in range(QT):
                            st_ = dve.bn_stats(stats[:, i, :], X[:, (b + sh) * QT + i, :])
                        st_.then_inc(stats_done, 1)
                        dve.wait_ge(stats_done, k)
                        dve.memset(carrier[:, :], 0.0)
                        for i in range(QT):
                            st_ = dve.bn_aggr(meanvar[:, i, :], stats[:, i, :])
                        st_.then_inc(agg_done, 1)
                        dve.wait_ge(agg_done, k)
                        dve.tensor_scalar(var_eps[:, :], meanvar[:, :, 1], EPS, None, ALU.add).then_inc(eps_done, 1)

                    def norm_apply(w, b, sh):
                        dve.wait_ge(rstd_done, norms("T" + w, b, sh))
                        for i in range(QT):
                            st_ = dve.tensor_scalar(xn[:, i, :], X[:, (b + sh) * QT + i, :], meanvar[:, i, 0:1],
                                                    rstd[:, i:i + 1], ALU.subtract, ALU.mult)
                        st_.then_inc(xn_done, 1)

                    def low(w, b, sh):
                        o = bank_of("T" + w, b, sh)
                        dve.wait_ge(high_done, norms("T" + w, b, sh))
                        dve.tensor_tensor(xT_lo[w][:, :], o, xT_hi[w][:, :].bitcast(F32), ALU.subtract
                                          ).then_inc(shared_read_dve, 1)

                    def gates(w, b, sh):
                        k = routes("L" + w, b, sh)
                        dve.wait_ge(shared_read_act, shared.read["act"]("L" + w, b, sh))
                        dve.tensor_reduce(top[:, :], logit[:, :, :], AX.X, ALU.max).then_inc(g_top, 1)
                        by_e = logit[:, :, :].unsqueeze(3).broadcast_to([P, QT, E, E])
                        by_j = logit[:, :, :].unsqueeze(2).broadcast_to([P, QT, E, E])
                        dve.tensor_tensor(gt[:, :, :, :], by_j, by_e, ALU.is_gt)
                        dve.wait_ge(g_top, k)
                        dve.tensor_tensor(shifted[:, :, :], logit[:, :, :],
                                          top[:, :].unsqueeze(2).broadcast_to([P, QT, E]),
                                          ALU.subtract).then_inc(shift_done, 1)
                        dve.tensor_tensor(ge[:, :, :, :], by_j, by_e, ALU.is_ge).then_inc(g_cmp, 1)
                        dve.wait_ge(g_cmp, k)
                        pairs = lambda a: a.rearrange("p t e j -> p t (e j)")
                        later, earlier = (ranks[:, n].rearrange("p e j -> p (e j)").unsqueeze(1).broadcast_to(
                            [P, QT, E * E]) for n in range(2))
                        dve.tensor_tensor(pairs(gt[:, :, :, :]), pairs(gt[:, :, :, :]), later, ALU.mult)
                        dve.tensor_tensor(pairs(ge[:, :, :, :]), pairs(ge[:, :, :, :]), earlier, ALU.mult).then_inc(g_mul, 1)
                        dve.wait_ge(g_mul, k)
                        dve.tensor_tensor(pairs(gt[:, :, :, :]), pairs(gt[:, :, :, :]), pairs(ge[:, :, :, :]),
                                          ALU.add).then_inc(g_add, 1)
                        dve.wait_ge(g_add, k)
                        dve.tensor_reduce(rank[:, :, :], gt[:, :, :, :], AX.X, ALU.add).then_inc(g_rank, 1)
                        dve.wait_ge(g_rank, k)
                        dve.tensor_scalar(taken[:, :, :], rank[:, :, :], TOPK - 0.5, 0.5, ALU.is_lt,
                                          ALU.mult).then_inc(g_take, 1)
                        dve.wait_ge(expo_done, k)
                        dve.tensor_reduce(total[:, :], expo[:, :, :], AX.X, ALU.add).then_inc(g_tot, 1)
                        dve.wait_ge(g_take, k)
                        dve.tensor_tensor(chosen[:, :, :], expo[:, :, :], taken[:, :, :], ALU.mult).then_inc(g_pick, 1)
                        dve.wait_ge(g_tot, k)
                        dve.reciprocal(inv_total[:, :], total[:, :]).then_inc(g_inv, 1)
                        dve.wait_ge(g_inv, k)
                        dve.wait_ge(g_pick, k)
                        dve.tensor_tensor(gate[w][:, :, :], chosen[:, :, :],
                                          inv_total[:, :].unsqueeze(2).broadcast_to([P, QT, E]),
                                          ALU.mult).then_inc(gate_done, 1)

                    def weigh_experts(w, b, sh, i, start):
                        if i == 0:
                            dve.wait_ge(gate_done, routes("L" + w, b, sh))
                        t, c = i // 2, i % 2
                        if c == 0 and not (start and t < 2):
                            dve.wait_ge(summed, tiles("Y" + w, b, sh, t, less=2))
                        o = bank_of("Y" + w, b, sh, i)
                        es = slice(c * E // 2, (c + 1) * E // 2)
                        dve.tensor_tensor(Z[:, t % 2, es, :], o.rearrange("p (e d) -> p e d", d=D),
                                          gate[w][:, t, es].unsqueeze(2).broadcast_to([P, E // 2, D]),
                                          ALU.mult).then_inc(shared_read_dve, 1)

                    def rotate(b, sh, p, start=False):
                        k, r = pair_no(b, sh, p), p % 2
                        for n, name in ((0, "Q"), (2, "K")):
                            o = bank_of(name, b, sh, p)
                            if n == 0 and not start:
                                dve.wait_ge(qk_done, k - 1)
                            dve.tensor_tensor(rot[:, r, n + 1, :], o, tables[:, n + 1, :], ALU.mult).then_inc(rotated, 1)
                            dve.tensor_tensor(rot[:, r, n, :], o, tables[:, n, :], ALU.mult).then_inc(shared_read_dve, 1)
                        dve.wait_ge(rotated, k * 2 + 2)
                        dve.memset(carrier[:, :], 0.0)
                        swap = [(n + ROPE // 2) % ROPE for n in range(ROPE)]
                        for n in (1, 3):
                            dve.stream_shuffle(rot[:, r, n, :], rot[:, r, n, :], mask=swap).then_inc(turned_half, 1)

                    def maxima(b, h):
                        k = head_no(b, 0, h)
                        for u, tiles_ in enumerate(SCORE_UNITS):
                            dve.wait_ge(scores_ready, k * 3 + u + 1)
                            for i in tiles_:
                                at = SCORE_AT[i][1]
                                mx = dve.tensor_reduce(negmax[:, h % 2, i:i + 1], flat[:, at:at + (i + 1) * P],
                                                       AX.X, ALU.max, negate=True)
                            mx.then_inc(max_done, 1)

                    def invert(b, sh, p):
                        k = pair_no(b, sh, p)
                        dve.wait_ge(exp_done, k * 6 + 6)
                        dve.reciprocal(inv_den[:, :, :], den[:, p % 2, :, :]).then_inc(inv_done, 1)
                        dve.wait_ge(inv_done, k + 1)
                        dve.tensor_copy(inv_wide[:, :, :].rearrange("p i (a d) -> p i a d", a=2),
                                        inv_den[:, :, :].unsqueeze(3).broadcast_to([P, QT, 2, DK])).then_inc(wide_done, 1)

                    def normalise(b, sh, p, start=False):
                        dve.wait_ge(pv_ready, pair_no(b, sh, p) + 1)
                        dve.wait_ge(shared_read_act, shared.read["act"]("R", b, sh, p))
                        if p == 0 and not start:
                            dve.wait_ge(shared_ready, shared.ready("O", b, sh - 1))
                        dve.tensor_tensor(OT[:, p, :], banks[:, O_BANK, :], R[:, :], ALU.mult).then_inc(o_done, 1)

                    def add_residual(b, sh):
                        o = bank_of("O", b, sh)
                        xb = X[:, bass.ds((b + sh) * QT, QT), :]
                        dve.tensor_tensor(xb, o.rearrange("p (t d) -> p t d", t=QT), xb, ALU.add).then_inc(shared_read_dve, 1)

                    def run(units, b, start=False):
                        for kind, sh, i in units:
                            if kind[0] == "T":
                                low(kind[1:], b, sh)
                            elif kind in ("L1", "L2"):
                                gates(kind[1:], b, sh)
                            elif kind[0] == "Y":
                                weigh_experts(kind[1:], b, sh, i, start)
                            elif kind == "O":
                                add_residual(b, sh)

                    def prologue():
                        dve.memset(Q_hi[:, :, :, :].bitcast(F32), 0.0).then_inc(padded, 1)
                        dve.memset(Q_lo[:, :, :, :].bitcast(F32), 0.0).then_inc(padded, 1)
                        norm_stats("1", 0, 0)
                        norm_apply("1", 0, 0)
                        ffn1 = PROLOGUE[:PROLOGUE.index(("T", 0, 0))]
                        run(ffn1, 0, True)
                        norm_stats("", 0, 0)
                        norm_apply("", 0, 0)
                        run(PROLOGUE[len(ffn1):], 0)
                        rotate(0, 0, 0, True)
                        rotate(0, 0, 1, True)

                    def body(b, first, last):
                        for p in range(NPAIR):
                            sh, pp = before(p)
                            if not (first and p == 0):
                                invert(b, sh, pp)
                            maxima(b, 2 * p)
                            run(extras(p, "mid", first, last), b)
                            if p == 0 and not last:
                                norm_stats("1", b, 1)
                            if p == 1 and not first:
                                norm_stats("2", b, -1)
                            if p == 5 and not last:
                                norm_stats("", b, 1)
                            if not (first and p == 0):
                                normalise(b, sh, pp, first)
                            maxima(b, 2 * p + 1)
                            if p == 0 and not last:
                                norm_apply("1", b, 1)
                            if p == 1 and not first:
                                norm_apply("2", b, -1)
                            if p == 5 and not last:
                                norm_apply("", b, 1)
                            run(extras(p, "end", first, last), b)
                            nsh, pn = after(p, 2)
                            if not (last and nsh):
                                rotate(b, nsh, pn)
                            run(extras(p, "late", first, last), b)

                    def epilogue():
                        invert(B - 1, 0, NPAIR - 1)
                        normalise(B - 1, 0, NPAIR - 1)
                        run(EPILOGUE[:1], B - 1)
                        norm_stats("2", B - 1, 0)
                        norm_apply("2", B - 1, 0)
                        run(EPILOGUE[1:], B - 1)

                    batches(dve, prologue, body, epilogue)

                @block.gpsimd
                def _(pool):
                    def norm_rstd(w, b, sh):
                        k = norms("T" + w, b, sh)
                        pool.wait_ge(eps_done, k)
                        pool.tensor_tensor(rstd[:, :], var_eps[:, :], minus_half[:, :], ALU.pow).then_inc(rstd_done, 1)

                    def sum_rotated(b, sh, p):
                        k, r = pair_no(b, sh, p), p % 2
                        for n in (0, 2):
                            pool.wait_ge(shared_read_dve, shared.read["dve"]("K" if n else "Q", b, sh, p))
                            pool.wait_ge(turned_half, k * 2 + n // 2 + 1)
                            pool.tensor_tensor(rot[:, r, n, :], rot[:, r, n, :], rot[:, r, n + 1, :], ALU.add).then_inc(qk_sum, 1)

                    def low_qk(b, sh, p):
                        k, r = pair_no(b, sh, p), p % 2
                        pool.wait_ge(qk_high, k * 2 + 1)
                        pool.tensor_tensor(K_lo[:, r, :], rot[:, r, 2, :], K_hi[:, r, :].bitcast(F32), ALU.subtract
                                           ).then_inc(q_low, 1)
                        pool.wait_ge(qk_high, k * 2 + 2)
                        pool.wait_ge(q_low, k * 2 + 1)
                        pool.tensor_tensor(Q_lo[0:DK, r, 0, :], rot[0:DK, r, 0, :], Q_hi[0:DK, r, 0, :].bitcast(F32),
                                           ALU.subtract).then_inc(q_low, 1)
                        pool.wait_ge(q_low, k * 2 + 2)
                        pool.tensor_tensor(Q_lo[DK:P, r, 1, :], rot[DK:P, r, 0, :], Q_hi[DK:P, r, 1, :].bitcast(F32),
                                           ALU.subtract).then_inc(qk_done, 1)
                        pool.wait_ge(qk_done, k + 1)

                    def add_up(w, b, sh, i):
                        k = tiles("Y" + w, b, sh, i, less=1) * 3
                        z = Z[:, i % 2, :, :]
                        pool.wait_ge(shared_read_dve, shared.read["dve"]("Y" + w, b, sh, 2 * i + 1))
                        pool.tensor_tensor(z[:, 0:4], z[:, 0:4], z[:, 4:8], ALU.add).then_inc(z_adds, 1)
                        pool.wait_ge(z_adds, k + 1)
                        pool.tensor_tensor(z[:, 0:2], z[:, 0:2], z[:, 2:4], ALU.add).then_inc(z_adds, 1)
                        pool.wait_ge(z_adds, k + 2)
                        pool.tensor_tensor(z[:, 0], z[:, 0], z[:, 1], ALU.add).then_inc(z_adds, 1)
                        pool.wait_ge(z_adds, k + 3)
                        x_t = X[:, (b + sh) * QT + i, :]
                        pool.tensor_tensor(x_t, x_t, z[:, 0], ALU.add).then_inc(summed, 1)

                    def run(units, b):
                        for kind, sh, i in units:
                            if kind[0] == "Y" and i % 2:
                                add_up(kind[1:], b, sh, i // 2)

                    def prologue():
                        norm_rstd("1", 0, 0)
                        run(PROLOGUE, 0)
                        norm_rstd("", 0, 0)
                        sum_rotated(0, 0, 0)
                        low_qk(0, 0, 0)
                        sum_rotated(0, 0, 1)

                    def body(b, first, last):
                        for p in range(NPAIR):
                            if p == 0 and not last:
                                norm_rstd("1", b, 1)
                            if p == 1 and not first:
                                norm_rstd("2", b, -1)
                            if p == 5 and not last:
                                norm_rstd("", b, 1)
                            nsh, pn = after(p, 1)
                            if not (last and nsh):
                                low_qk(b, nsh, pn)
                            run(extras(p, "mid", first, last), b)
                            nsh, pn = after(p, 2)
                            if not (last and nsh):
                                sum_rotated(b, nsh, pn)
                            run(extras(p, "end", first, last), b)

                    def epilogue():
                        norm_rstd("2", B - 1, 0)
                        run(EPILOGUE, B - 1)

                    batches(pool, prologue, body, epilogue)

                @block.sync
                def _(sp):
                    o = out.rearrange("b (t p) d -> p b t d", p=P)

                    def store(b, sh):
                        sp.wait_ge(summed, tiles("Y2", b, sh, QT - 1))
                        sp.dma_start(o[:, bass.ds(b + sh, 1), :, :], X[:, bass.ds((b + sh) * QT, QT), :].rearrange(
                            "p (a t) d -> p a t d", a=1)).then_inc(out_done, 16)

                    with sp.Fori(1, B - 1) as b:
                        store(b, -1)
                    store(B - 1, -1)
                    store(B - 1, 0)
                    sp.wait_ge(out_done, 16 * B)


def shape_tables():
    inv_freq = (1.0 / np.power(np.float32(6000.0), np.arange(0, ROPE, 2, dtype=np.float32) / np.float32(ROPE))).astype(np.float32)
    angle = np.outer(np.arange(S, dtype=np.float32), inv_freq).astype(np.float32)
    cos, sin = np.cos(angle).astype(np.float32).T, np.sin(angle).astype(np.float32).T
    c = np.ones((DK, S), np.float32)
    s = np.zeros((DK, S), np.float32)
    c[0:16], c[16:32] = cos, cos
    s[0:16], s[16:32] = sin, -sin
    c, s = np.concatenate([c, c]), np.concatenate([s, s])
    scale = np.float32(1.0 / np.sqrt(DK))
    e = np.arange(E)
    rank = np.stack([e[None, :] > e[:, None], e[None, :] < e[:, None]]).astype(np.float32)
    mask = np.where(np.arange(P)[None, :] > np.arange(P)[:, None], np.float32(-1e30), np.float32(0))
    return {
        "cos_q": c * scale, "sin_q": s * scale, "cos_k": c, "sin_k": s, "ident": np.eye(P, dtype=np.float32),
        "rank": np.ascontiguousarray(np.broadcast_to(rank, (P, 2, E, E))), "mask": mask.astype(np.float32),
    }


_INS = ['L0_attn_x', 'L0_attn_W_qkv', 'L0_attn_W_o', 'L0_ffn_Wr', 'L0_ffn_Wi', 'L0_ffn_Wo']


def kernel(**inputs):
    import concourse.bacc as _bacc
    from concourse.bass_utils import run_bass_kernel_spmd as _run

    nc = _bacc.Bacc("TRN2", target_bir_lowering=False, num_devices=1)
    arrays, args = {}, []
    for name, a in [(n, inputs[n]) for n in _INS] + list(shape_tables().items()):
        a = np.ascontiguousarray(a)
        arrays[f"in_{name}_dram"] = a
        args.append(nc.dram_tensor(f"in_{name}_dram", a.shape, mybir.dt.from_np(a.dtype), kind="ExternalInput").ap())
    args.append(nc.dram_tensor("out_dram", (B, S, D), F32, kind="ExternalOutput").ap())
    build(nc, *args)
    r = _run(nc, [arrays], core_ids=[0])
    return r.results[0]["out_dram"]
```

```python
import concourse.bass as bass
from concourse import mybir
from contextlib import ExitStack
import numpy as np

F32 = mybir.dt.float32
F32R = mybir.dt.float32r
BF16 = mybir.dt.bfloat16
ALU = mybir.AluOpType
ACT = mybir.ActivationFunctionType
AX = mybir.AxisListType

P = 128
B, S, D = 16, 512, 128
H, DK = 16, 64
E = 8
TOPK = 2
GATE_SCALE = 0.5
EPS = 1e-5
ROPE = DK // 2
QT = S // P
NPAIR = H // 2
OWN = [slice(0, DK), slice(DK, P)]
BANK = 512

SCORE_AT = {3: (0, 0), 2: (1, 512), 0: (1, 896), 1: (2, 1024)}
SCORE_UNITS = [[3], [2, 0], [1]]
PROBT_AT = {2: (0, 0), 0: (1, 256), 1: (2, 768), 3: (2, 1152)}
PROBT_UNITS = [[2], [0], [1, 3]]
PROBT_WIDTH = [256, 512, 512]
PROB_COLS = 1280


EXTRAS = {
    (0, "end"): [("V", 0, 4), ("V", 0, 5)],
    (0, "late"): [("O", -1, 3), ("T1", 1, 0)],
    (1, "end"): [("LT1", 1, 0), ("V", 0, 6)],
    (1, "late"): [("V", 0, 7), ("T2", -1, 0)],
    (2, "mid"): [("L1", 1, 0)],
    (2, "end"): [("Y1", 1, 0), ("Y1", 1, 1)],
    (2, "late"): [("LT2", -1, 0)],
    (3, "mid"): [("O", 0, 0), ("Y1", 1, 2)],
    (3, "end"): [("Y1", 1, 3)],
    (3, "late"): [("Y1", 1, 4)],
    (4, "mid"): [("Y1", 1, 5)],
    (4, "end"): [("Y1", 1, 6), ("Y1", 1, 7), ("L2", -1, 0)],
    (4, "late"): [("O", 0, 1)],
    (5, "end"): [("Y2", -1, 0), ("Y2", -1, 1)],
    (5, "late"): [("T", 1, 0)],
    (6, "end"): [("Y2", -1, 2), ("Y2", -1, 3), ("Y2", -1, 4)],
    (6, "late"): [("V", 1, 0), ("O", 0, 2)],
    (7, "mid"): [("Y2", -1, 5), ("V", 1, 1)],
    (7, "end"): [("Y2", -1, 6), ("Y2", -1, 7)],
    (7, "late"): [("V", 1, 2), ("V", 1, 3)],
}
PROLOGUE = ([("T1", 0, 0), ("LT1", 0, 0), ("L1", 0, 0)] + [("Y1", 0, i) for i in range(2 * QT)] + [("T", 0, 0)]
            + [("Q", 0, 0), ("K", 0, 0)] + [("V", 0, j) for j in range(QT)] + [("Q", 0, 1), ("K", 0, 1)])
EPILOGUE = [("O", 0, NPAIR // 2 - 1), ("T2", 0, 0), ("LT2", 0, 0), ("L2", 0, 0)] + [("Y2", 0, i) for i in range(2 * QT)]


VECTOR = {
    (0, "a"): [("S1", 1)],
    (0, "d"): [("A1", 1)],
    (1, "b"): [("S2", -1)],
    (1, "e"): [("A2", -1)],
    (2, "b"): [("G1", 1)],
    (2, "c"): [("P1", 1)],
    (4, "f"): [("G2", -1)],
    (5, "b"): [("S", 1), ("P2", -1)],
    (5, "d"): [("A", 1)],
}
ROUTE_EXP = {
    (2, "mid"): [("L1", 1)],
    (5, "mid"): [("L2", -1)],
}


def jobs(table, p, slot, first, last):
    return [u for u in table.get((p, slot), ()) if not (first and u[1] < 0) and not (last and u[1] > 0)]


def extras(p, slot, first, last):
    return [u for u in EXTRAS.get((p, slot), ()) if not (first and u[1] < 0) and not (last and u[1] > 0)]


def before(p):
    return (0, p - 1) if p else (-1, NPAIR - 1)


def after(p, ahead):
    return (0, p + ahead) if p + ahead < NPAIR else (1, p + ahead - NPAIR)


def whole_order():
    order = [(k, b, i) for k, b, i in PROLOGUE]
    for b in range(B):
        for p in range(NPAIR):
            order += [(k, b + sh, i) for k, sh, i in extras(p, "mid", b == 0, b == B - 1)]
            sh, pn = after(p, 2)
            if b + sh < B:
                order += [("Q", b + sh, pn), ("K", b + sh, pn)]
            sh, pp = before(p)
            if b + sh >= 0:
                order.append(("R", b + sh, pp))
            order += [(k, b + sh, i) for k, sh, i in extras(p, "end", b == 0, b == B - 1)]
            order += [(k, b + sh, i) for k, sh, i in extras(p, "late", b == 0, b == B - 1)]
    return order + [("R", B - 1, NPAIR - 1)] + [(k, B - 1, i) for k, _, i in EPILOGUE]


class Counts:

    MID = 5

    def __init__(self, events):
        self.at = {e: n + 1 for n, e in enumerate(events)}

    def __call__(self, kind, b, shift, index=0, less=0):
        if isinstance(b, int):
            return self.at[(kind, b + shift, index)] - less
        one, two = (self.at[(kind, m + shift, index)] for m in (self.MID, self.MID + 1))
        return b * (two - one) + (one - less - self.MID * (two - one))


READER = {"V": "act", "R": "act", "LT1": "act", "LT2": "act", "L1": "act", "L2": "act"}


class Banks:

    def __init__(self, units):
        self.units = units
        self.ready = Counts(units)
        self.read = {who: Counts([u for u in units if READER.get(u[0], "dve") == who]) for who in ("act", "dve")}

    def place(self, kind, b, shift, index=0):
        return self.ready.at[(kind, (b if isinstance(b, int) else Counts.MID) + shift, index)] - 1

    def bank(self, *unit):
        return self.place(*unit) % 2

    def reader(self, kind):
        return READER.get(kind, "dve")

    def free(self, kind, b, shift, index=0):
        n = self.place(kind, b, shift, index)
        if n < 2:
            return None
        k, bb, i = self.units[n - 2]
        who = self.reader(k)
        if isinstance(b, int):
            return who, self.read[who](k, bb, 0, i)
        return who, self.read[who](k, b, bb - Counts.MID, i)


def build(nc, x, w_qkv, w_o, w_r, w_i, w_out, cos_q, sin_q, cos_k, sin_k, ident_d, rank_d, mask_d, out):
    outer = ExitStack()
    with outer:
        def sb(name, shape, dt=F32, stack=outer):
            return stack.enter_context(nc.sbuf_tensor(name, shape, dt))

        def sem(name, stack=outer):
            return stack.enter_context(nc.semaphore(name))

        X = sb("X", [P, B * QT, D])
        W_hi = sb("W_hi", [P, 3, H * DK], F32R)
        W_lo = sb("W_lo", [P, 3, H * DK], F32R)
        WoT = sb("WoT", [P, NPAIR, D])
        M_hi = sb("M_hi", [P, E * D], F32R)
        M_lo = sb("M_lo", [P, E * D], F32R)
        Wr_hi = sb("Wr_hi", [P, P], F32R)
        Wr_lo = sb("Wr_lo", [P, P], F32R)
        tables = sb("tables", [P, 4, S])
        ident = sb("ident", [P, P])
        ident_b = sb("ident_b", [P, P], BF16)
        mask_b = sb("mask_b", [P, 2, P], BF16)
        earlier = sb("earlier", [P, E, E])
        rank_limit = sb("rank_limit", [P, E])
        minus_half = sb("minus_half", [P, QT])
        banks = outer.enter_context(nc.psum_tensor("banks", [P, 8, BANK], F32))
        flat = banks[:, :, :].rearrange("p a b -> p (a b)")

        with ExitStack() as st:
            def asb(name, shape, dt=F32):
                return sb(name, shape, dt, st)

            def asem(name):
                return sem(name, st)

            order = whole_order()
            shared = Banks(order)
            norms = Counts([u for u in order if u[0] in ("T", "T1", "T2")])
            routes = Counts([u for u in order if u[0] in ("L1", "L2")])
            vector_sums = [("Y1", 0, 1), ("Y1", 0, 3), ("Y2", B - 1, 1), ("Y2", B - 1, 3)]
            summed_tiles = [(k, b, i // 2) for k, b, i in order if k in ("Y1", "Y2") and i % 2]
            tiles = Counts([u for u in summed_tiles if u not in vector_sums])
            vector_tiles = Counts(vector_sums)

            stats = asb("stats", [P, QT, 6])
            meanvar = asb("meanvar", [P, QT, 2])
            var_eps = asb("var_eps", [P, QT])
            rstd = asb("rstd", [P, QT])
            carrier = asb("carrier", [P, 4])
            xn = asb("xn", [P, QT, D])
            xT_hi = {w: asb(f"xT{w}_hi", [P, S], F32R) for w in ("", "1", "2")}
            xT_lo = {w: asb(f"xT{w}_lo", [P, S], F32R) for w in ("", "1", "2")}
            logitT = asb("logitT", [P, S])
            logit = asb("logit", [P, QT, E])
            top = asb("top", [P, QT])
            shifted = asb("shifted", [P, QT, E])
            expo = asb("expo", [P, QT, E])
            total = asb("total", [P, QT])
            inv_total = asb("inv_total", [P, QT])
            ge = asb("ge", [P, QT, E, E])
            row = asb("row", [P, QT, E])
            col = asb("col", [P, QT, E])
            rank = asb("rank", [P, QT, E])
            twice = asb("twice", [P, QT])
            taken = asb("taken", [P, QT, E])
            chosen = asb("chosen", [P, QT, E])
            gate = {w: asb(f"gate{w}", [P, QT, E]) for w in ("1", "2")}
            Z = asb("Z", [P, 2, E, D])
            V = asb("V", [P, QT, H * DK])
            rot = asb("rot", [P, 2, 4, S])
            Q_hi = asb("Q_hi", [P, 2, 2, S], F32R)
            Q_lo = asb("Q_lo", [P, 2, 2, S], F32R)
            K_hi = asb("K_hi", [P, S], F32R)
            K_lo = asb("K_lo", [P, S], F32R)
            K_both = asb("K_both", [P, 2, 2, S], F32R)
            probs = asb("probs", [P, PROB_COLS])
            probsT = asb("probsT", [P, 2, PROB_COLS])
            negmax = asb("negmax", [P, 2, QT])
            den = asb("den", [P, 2, QT, 2])
            inv_den = asb("inv_den", [P, QT, 2])
            inv_wide = asb("inv_wide", [P, QT, P])
            R = asb("R", [P, S])
            OT = asb("OT", [P, NPAIR, S])

            wn = V[:, :, :].rearrange("p j c -> p (j c)")[:, 0:3 * H * DK].rearrange("p (t m) -> p t m", m=P)
            spare = probsT[:, :, :].rearrange("p a c -> p (a c)")
            win = spare[:, 0:E * D].rearrange("p (e h) -> p e h", e=E)
            woutn = spare[:, E * D:2 * E * D].rearrange("p (e d) -> p e d", e=E)
            wrn, mask_f = spare[:, 2 * E * D:2 * E * D + P], spare[:, 2 * E * D + P:2 * E * D + 2 * P]
            spare_O = OT[:, :, :].rearrange("p a c -> p (a c)")
            won, wit = spare_O[:, 0:H * DK], spare_O[:, H * DK:H * DK + E * D].rearrange("p (e d) -> p e d", e=E)
            NW = 6
            W_BANK = [0, 1, 6, 7, 2, 5]
            M_BANK = [2, 5]
            x_first_in, x_in, ident_in, mask_in, rank_in, tables_in, w_in, wo_in, wi_in, wout_in, wr_in = (
                asem(n) for n in ("x_first_in", "x_in", "ident_in", "mask_in", "rank_in", "tables_in", "w_in", "wo_in",
                                  "wi_in", "wout_in", "wr_in"))
            turned, hi_done, lo_done, cast, filled = (asem(n) for n in ("turned", "hi_done", "lo_done", "cast", "filled"))
            FIRST = [("T1", 0, 0), ("LT1", 0, 0), ("L1", 0, 0), ("W", 0, 0), ("W", 0, 1), ("W", 0, 2), ("Y1", 0, 0),
                     ("Y1", 0, 1), ("W", 0, 3), ("Y1", 0, 2), ("Y1", 0, 3), ("W", 0, 4), ("Y1", 0, 4), ("Y1", 0, 5),
                     ("W", 0, 5), ("WO", 0, 0), ("Y1", 0, 6), ("Y1", 0, 7), ("WO", 0, 1)]
            THEN = PROLOGUE[PROLOGUE.index(("T", 0, 0)):]

            shared_ready, shared_read_act, shared_read_dve = (
                asem(n) for n in ("shared_ready", "shared_read_act", "shared_read_dve"))
            stats_done, agg_done, eps_done, rstd_done, xn_done, high_done = (
                asem(n) for n in ("stats_done", "agg_done", "eps_done", "rstd_done", "xn_done", "high_done"))
            g_top, g_cmp, g_mul, g_add, g_rank, g_take, g_tot, g_inv, g_pick, g_twice = (
                asem(n) for n in ("g_top", "g_cmp", "g_mul", "g_add", "g_rank", "g_take", "g_tot", "g_inv", "g_pick", "g_twice"))
            shift_done, expo_done, gate_done, z_done, z_adds, summed, vector_adds, vector_summed, out_done = (
                asem(n) for n in ("shift_done", "expo_done", "gate_done", "z_done", "z_adds", "summed", "vector_adds", "vector_summed", "out_done"))
            padded, rotated, turned_half, qk_sum, qk_high, low_done, qk_done, k_hi_moved, k_lo_moved, q_moved = (
                asem(n) for n in ("padded", "rotated", "turned_half", "qk_sum", "qk_high", "low_done", "qk_done", "k_hi_moved", "k_lo_moved", "q_moved"))
            scores_ready, max_done, exp_done, pt_ready, pt_copied = (
                asem(n) for n in ("scores_ready", "max_done", "exp_done", "pt_ready", "pt_copied"))
            pv_ready, inv_done, wide_done, o_done = (
                asem(n) for n in ("pv_ready", "inv_done", "wide_done", "o_done"))
            SHARED_BANK, O_BANK = 3, 7
            tokens = x.rearrange("b (t p) d -> p (b t) d", p=P)
            PROBT_COL = [3 * BANK - PROBT_WIDTH[0], 5 * BANK, 6 * BANK]

            def head_no(b, shift, h):
                return (b + shift) * H + h

            def pair_no(b, shift, p):
                return (b + shift) * NPAIR + p

            def batches(engine, prologue, body, epilogue):
                prologue()
                body(0, True, False)
                with engine.Fori(1, B - 1) as b:
                    body(b, False, False)
                body(B - 1, False, True)
                epilogue()

            with nc.Block() as block:

                @block.tensor
                def _(pe):
                    def claim(*unit):
                        free = shared.free(*unit)
                        if free:
                            pe.wait_ge(shared_read_act if free[0] == "act" else shared_read_dve, free[1])
                        return banks[:, SHARED_BANK + shared.bank(*unit), :]

                    def split_product(o, l_hi, l_lo, r_hi, r_lo):
                        pe.matmul(o, l_hi, r_hi, start=True, stop=False)
                        pe.matmul(o, l_hi, r_lo, start=False, stop=False)
                        return pe.matmul(o, l_lo, r_hi, start=False, stop=True)

                    def both_parts(w, b, sh):
                        pe.wait_ge(shared_read_dve, shared.read["dve"]("T" + w, b, sh))

                    def turn(w, b, sh):
                        o = claim("T" + w, b, sh)
                        pe.wait_ge(xn_done, norms("T" + w, b, sh))
                        for i in range(QT):
                            mm = pe.transpose(o[:, i * P:(i + 1) * P], xn[:, i, :], ident[:, :])
                        mm.then_inc(shared_ready, 1)

                    def logits_T(w, b, sh):
                        o = claim("LT" + w, b, sh)
                        both_parts(w, b, sh)
                        split_product(o, Wr_hi[:, :], Wr_lo[:, :], xT_hi[w][:, :], xT_lo[w][:, :]).then_inc(shared_ready, 1)

                    def logits(w, b, sh):
                        o = claim("L" + w, b, sh)
                        pe.wait_ge(shared_read_act, shared.read["act"]("LT" + w, b, sh))
                        for i in range(QT):
                            mm = pe.transpose(o[:, i * P:(i + 1) * P], logitT[:, i * P:(i + 1) * P], ident[:, :])
                        mm.then_inc(shared_ready, 1)

                    def experts(w, b, sh, i):
                        o = claim("Y" + w, b, sh, i)
                        tok, cols = slice(i // 2 * P, (i // 2 + 1) * P), slice(i % 2 * BANK, (i % 2 + 1) * BANK)
                        split_product(o, xT_hi[w][:, tok], xT_lo[w][:, tok], M_hi[:, cols], M_lo[:, cols]
                                      ).then_inc(shared_ready, 1)

                    def values(b, sh, i):
                        o = claim("V", b, sh, i)
                        half, j = i // QT, i % QT
                        cols, tok = slice(half * BANK, (half + 1) * BANK), slice(j * P, (j + 1) * P)
                        both_parts("", b, sh)
                        split_product(o, xT_hi[""][:, tok], xT_lo[""][:, tok], W_hi[:, 2, cols], W_lo[:, 2, cols]
                                      ).then_inc(shared_ready, 1)

                    def project(b, sh, p):
                        cols = slice(p * P, (p + 1) * P)
                        both_parts("", b, sh)
                        for name, w in (("Q", 0), ("K", 1)):
                            o = claim(name, b, sh, p)
                            split_product(o, W_hi[:, w, cols], W_lo[:, w, cols], xT_hi[""][:, :], xT_lo[""][:, :]
                                          ).then_inc(shared_ready, 1)

                    def scores(b, h, units, start=False):
                        r, a, k = (h // 2) % 2, h % 2, head_no(b, 0, h)
                        if a == 0 and units[0] == 0:
                            pair = pair_no(b, 0, h // 2)
                            pe.wait_ge(qk_done, pair + 1)
                            pe.wait_ge(q_moved, (pair + 1) * 2 * 16)
                            pe.wait_ge(k_hi_moved, (pair + 1) * 2 * 16)
                            pe.wait_ge(k_lo_moved, (pair + 1) * 2 * 16)
                        for u in units:
                            if not start:
                                if u == 2:
                                    pe.wait_ge(pt_copied, k * 3 - 2)
                                else:
                                    pe.wait_ge(exp_done, k * 3 - 2 + u)
                            at, masks = SCORE_AT[SCORE_UNITS[u][0]][1] + SCORE_UNITS[u][0] * P, len(SCORE_UNITS[u])
                            pe.matmul(flat[:, at:at + masks * P], ident_b[:, :],
                                      mask_b[:, 0:masks, :].rearrange("p a b -> p (a b)"),
                                      start=True, stop=False, skip_group_check=True)
                            for i in SCORE_UNITS[u]:
                                at, n, q = SCORE_AT[i][1], (i + 1) * P, slice(i * P, (i + 1) * P)
                                pe.matmul(flat[:, at:at + n], Q_hi[:, r, a, q], K_both[:, r, a, 0:n],
                                          start=False, stop=False, skip_group_check=True)
                                mm = pe.matmul(flat[:, at:at + n], Q_lo[:, r, a, q], K_both[:, r, a, 0:n],
                                               start=False, stop=(i == SCORE_UNITS[u][-1]), skip_group_check=True)
                            mm.then_inc(scores_ready, 1)

                    def turn_probs(b, sh, h, start=False):
                        k = head_no(b, sh, h)
                        pe.wait_ge(exp_done, k * 3 + 3)
                        for u, tiles_ in enumerate(PROBT_UNITS):
                            if not start:
                                pe.wait_ge(pt_copied, k * 3 + u - 2)
                            col = PROBT_COL[u]
                            for j in tiles_:
                                for i in range(j, QT):
                                    at = SCORE_AT[i][1] + j * P
                                    mm = pe.transpose(flat[:, col:col + P], probs[:, at:at + P], ident[:, :])
                                    col += P
                            mm.then_inc(pt_ready, 1)

                    def next_head(b, h, start=False):
                        scores(b, h, (0, 1))
                        turn_probs(b, 0 if h else -1, (h - 1) % H, start)
                        scores(b, h, (2,))

                    def weigh_values(b, sh, p, start=False):
                        k = pair_no(b, sh, p)
                        pe.wait_ge(pt_copied, k * 6 + 6)
                        if p in (0, NPAIR // 2):
                            pe.wait_ge(shared_read_act, shared.read["act"]("V", b, sh, QT - 1 if p == 0 else 2 * QT - 1))
                        if not start:
                            pe.wait_ge(o_done, k)
                        for j in range(QT):
                            at = PROBT_AT[j][1]
                            for a in range(2):
                                hd = 2 * p + a
                                mm = pe.matmul(banks[a * DK:(a + 1) * DK, O_BANK, j * P:S],
                                               V[:, j, hd * DK:(hd + 1) * DK],
                                               probsT[:, a, at:at + S - j * P], start=(j == 0), stop=(j == QT - 1))
                        mm.then_inc(pv_ready, 1)

                    def spread_den(b, sh, p):
                        o = claim("R", b, sh, p)
                        pe.wait_ge(wide_done, pair_no(b, sh, p) + 1)
                        for i in range(QT):
                            mm = pe.transpose(o[:, i * P:(i + 1) * P], inv_wide[:, i, :], ident[:, :])
                        mm.then_inc(shared_ready, 1)

                    def out_project(b, sh, part):
                        o = claim("O", b, sh, part)
                        pairs = (2 * part, 2 * part + 1)
                        pe.wait_ge(o_done, pair_no(b, sh, pairs[1]) + 1)
                        for i in range(QT):
                            for p in pairs:
                                mm = pe.matmul(o[:, i * P:(i + 1) * P], OT[:, p, i * P:(i + 1) * P], WoT[:, p, :],
                                               start=(p == pairs[0]), stop=(p == pairs[1]))
                        mm.then_inc(shared_ready, 1)

                    def run(units, b):
                        for kind, sh, i in units:
                            if kind[0] == "T":
                                turn(kind[1:], b, sh)
                            elif kind[:2] == "LT":
                                logits_T(kind[2:], b, sh)
                            elif kind[0] == "L":
                                logits(kind[1:], b, sh)
                            elif kind[0] == "Y":
                                experts(kind[1:], b, sh, i)
                            elif kind == "V":
                                values(b, sh, i)
                            elif kind == "O":
                                out_project(b, sh, i)
                            elif kind == "Q":
                                project(b, sh, i)

                    def turn_weights(g):
                        for a in range(4):
                            mm = pe.transpose(banks[:, W_BANK[g], a * P:(a + 1) * P], wn[:, 4 * g + a, :], ident[:, :])
                        mm.then_inc(turned, 1)

                    def turn_w_out(g):
                        pe.wait_ge(lo_done, 3 + 2)
                        for a in range(4):
                            mm = pe.transpose(banks[:, g, a * P:(a + 1) * P],
                                              won[:, (4 * g + a) * P:(4 * g + a + 1) * P], ident[:, :])
                        mm.then_inc(turned, 1)

                    def prologue():
                        pe.wait_ge(ident_in, 16)
                        pe.wait_ge(wi_in, 16)
                        for g in range(2):
                            for a in range(4):
                                mm = pe.transpose(banks[:, g, a * P:(a + 1) * P], win[:, 4 * g + a, :], ident[:, :])
                            mm.then_inc(turned, 1)
                        pe.wait_ge(wout_in, 16)
                        for g in range(2):
                            pe.wait_ge(hi_done, 1 + g + 1)
                            for a in range(4):
                                e = 4 * g + a
                                mm = pe.matmul(banks[:, M_BANK[g], a * P:(a + 1) * P], wit[:, e, :], woutn[:, e, :],
                                               start=True, stop=True)
                            mm.then_inc(turned, 1)
                        pe.wait_ge(lo_done, 3)
                        for unit in FIRST:
                            if unit[0] == "W":
                                if unit[2] == 0:
                                    pe.wait_ge(w_in, 16)
                                turn_weights(unit[2])
                            elif unit[0] == "WO":
                                pe.wait_ge(wo_in, 16)
                                turn_w_out(unit[2])
                            else:
                                run([unit], 0)
                        pe.wait_ge(hi_done, 5 + NW + 2)
                        pe.wait_ge(lo_done, 3 + NW)
                        pe.wait_ge(cast, 2)
                        run(THEN, 0)
                        pe.wait_ge(padded, 1)

                    def body(b, first, last):
                        for p in range(NPAIR):
                            sh, pp = before(p)
                            started = not (first and p == 0)
                            if started:
                                next_head(b, 2 * p)
                            else:
                                scores(b, 0, (0, 1, 2), True)
                            run(extras(p, "mid", first, last), b)
                            nsh, pn = after(p, 2)
                            if not (last and nsh):
                                project(b, nsh, pn)
                            if started:
                                weigh_values(b, sh, pp, first and p == 1)
                                spread_den(b, sh, pp)
                            next_head(b, 2 * p + 1, not started)
                            run(extras(p, "end", first, last), b)
                            run(extras(p, "late", first, last), b)

                    def epilogue():
                        turn_probs(B - 1, 0, H - 1)
                        weigh_values(B - 1, 0, NPAIR - 1)
                        spread_den(B - 1, 0, NPAIR - 1)
                        run(EPILOGUE, B - 1)

                    batches(pe, prologue, body, epilogue)

                @block.scalar
                def _(act):
                    def bank_of(*unit):
                        act.wait_ge(shared_ready, shared.ready(*unit))
                        return banks[:, SHARED_BANK + shared.bank(*unit), :]

                    def high(w, b, sh):
                        act.activation(xT_hi[w][:, :], bank_of("T" + w, b, sh), ACT.Copy).then_inc(high_done, 1)

                    def copy_logits_T(w, b, sh):
                        act.activation(logitT[:, :], bank_of("LT" + w, b, sh), ACT.Copy).then_inc(shared_read_act, 1)

                    def copy_logits(w, b, sh):
                        o = bank_of("L" + w, b, sh).rearrange("p (t n) -> p t n", n=P)[:, :, 0:E]
                        act.activation(logit[:, :, :], o, ACT.Copy).then_inc(shared_read_act, 1)

                    def route_exp(w, b, sh):
                        act.wait_ge(shift_done, routes("L" + w, b, sh))
                        act.activation(expo[:, :, :], shifted[:, :, :], ACT.Exp).then_inc(expo_done, 1)

                    def values(b, sh, i, start):
                        half, j = i // QT, i % QT
                        o = bank_of("V", b, sh, i)
                        if j == 0 and not start:
                            act.wait_ge(pv_ready, pair_no(b, sh - 1, (NPAIR // 2) * (half + 1) - 1) + 1)
                        act.activation(V[:, j, half * BANK:(half + 1) * BANK], o, ACT.Copy).then_inc(shared_read_act, 1)

                    def exps(b, h, units):
                        k, p = head_no(b, 0, h), h // 2
                        for u in units:
                            tiles_ = SCORE_UNITS[u]
                            act.wait_ge(max_done, k * 3 + u + 1)
                            for i in tiles_:
                                at = SCORE_AT[i][1]
                                cols = slice(at, at + (i + 1) * P)
                                ex = act.activation(probs[:, cols], flat[:, cols], ACT.Exp,
                                                    bias=negmax[:, h % 2, i:i + 1],
                                                    accum_out=den[:, p % 2, i, h % 2:h % 2 + 1])
                            ex.then_inc(exp_done, 1)

                    def copy_pt(b, sh, h, units=(0, 1, 2)):
                        k = head_no(b, sh, h)
                        for u in units:
                            n, at = PROBT_WIDTH[u], sum(PROBT_WIDTH[:u])
                            act.wait_ge(pt_ready, k * 3 + u + 1)
                            act.activation(probsT[:, h % 2, at:at + n],
                                           flat[:, PROBT_COL[u]:PROBT_COL[u] + n], ACT.Copy).then_inc(pt_copied, 1)

                    def copy_r(b, sh, p, start=False):
                        o = bank_of("R", b, sh, p)
                        if not start:
                            act.wait_ge(o_done, pair_no(b, sh, p))
                        act.activation(R[:, :], o, ACT.Copy).then_inc(shared_read_act, 1)

                    def high_k(b, sh, p, start=False):
                        k, r = pair_no(b, sh, p), p % 2
                        act.wait_ge(qk_sum, k * 2 + 2)
                        if not (start and p == 0):
                            act.wait_ge(k_hi_moved, k * 2 * 16)
                            act.wait_ge(low_done, k * 2 - 1)
                        if not start:
                            act.wait_ge(scores_ready, k * 6 - 6)
                        act.activation(K_hi[:, :], rot[:, r, 2, :], ACT.Copy).then_inc(qk_high, 1)

                    def high_q(b, sh, p, heads=(0, 1)):
                        r = p % 2
                        for a in heads:
                            act.activation(Q_hi[OWN[a], r, a, :], rot[OWN[a], r, 0, :], ACT.Copy).then_inc(qk_high, 1)

                    def run(units, b, first=False):
                        for kind, sh, i in units:
                            if kind[0] == "T":
                                high(kind[1:], b, sh)
                            elif kind[:2] == "LT":
                                copy_logits_T(kind[2:], b, sh)
                            elif kind[0] == "L":
                                copy_logits(kind[1:], b, sh)
                            elif kind == "V":
                                values(b, sh, i, first and sh == 0)

                    def prologue():
                        act.dma_start(win, w_i.rearrange("e d h -> d e h")).then_inc(wi_in, 16)
                        act.dma_start(X[:, 0:QT, :], tokens[:, 0:QT, :]).then_inc(x_first_in, 16)
                        act.wait_ge(wr_in, 16)
                        act.activation(Wr_hi[:, :], wrn, ACT.Copy).then_inc(hi_done, 1)
                        for g in range(2):
                            act.wait_ge(turned, g + 1)
                            act.activation(wit[:, 4 * g:4 * g + 4, :], banks[:, g, :].rearrange("p (a b) -> p a b", a=4),
                                           ACT.Copy).then_inc(hi_done, 1)
                        for g in range(2):
                            act.wait_ge(turned, 2 + g + 1)
                            act.activation(M_hi[:, g * BANK:(g + 1) * BANK], banks[:, M_BANK[g], :], ACT.Copy
                                           ).then_inc(hi_done, 1)
                        for unit in FIRST:
                            g = unit[2]
                            if unit[0] == "W":
                                act.wait_ge(turned, 4 + g + 1)
                                act.activation(W_hi[:, g // 2, (g % 2) * BANK:(g % 2 + 1) * BANK], banks[:, W_BANK[g], :],
                                               ACT.Copy).then_inc(hi_done, 1)
                            elif unit[0] == "WO":
                                act.wait_ge(turned, 4 + NW + g + 1)
                                act.activation(WoT[:, 4 * g:4 * g + 4, :], banks[:, g, :].rearrange(
                                    "p (a b) -> p a b", a=4), ACT.Copy).then_inc(hi_done, 1)
                            else:
                                run([unit], 0, True)
                                if unit[0] == "L1":
                                    route_exp("1", 0, 0)
                        run(THEN, 0, True)
                        high_k(0, 0, 0, True)
                        high_q(0, 0, 0)

                    def body(b, first, last):
                        for p in range(NPAIR):
                            sh, pp = before(p)
                            started = not (first and p == 0)
                            nsh, pn = after(p, 1)
                            more = not (last and nsh)
                            if started:
                                copy_pt(b, sh, 2 * pp + 1, (0, 1, 2))
                            exps(b, 2 * p, (0,))
                            if more:
                                high_k(b, nsh, pn, not started)
                            run(extras(p, "mid", first, last), b, first)
                            exps(b, 2 * p, (1, 2))
                            if more:
                                high_q(b, nsh, pn, (0,))
                            for unit, ush in jobs(ROUTE_EXP, p, "mid", first, last):
                                route_exp(unit[1:], b, ush)
                            if more:
                                high_q(b, nsh, pn, (1,))
                            if started:
                                copy_r(b, sh, pp, first and p == 1)
                            copy_pt(b, 0, 2 * p, (0, 1, 2))
                            exps(b, 2 * p + 1, (0,))
                            for unit, ush in jobs(ROUTE_EXP, p, "end", first, last):
                                route_exp(unit[1:], b, ush)
                            run(extras(p, "end", first, last), b, first)
                            exps(b, 2 * p + 1, (1, 2))
                            run(extras(p, "late", first, last), b, first)

                    def epilogue():
                        copy_pt(B - 1, 0, H - 1)
                        copy_r(B - 1, 0, NPAIR - 1)
                        run(EPILOGUE, B - 1)
                        route_exp("2", B - 1, 0)

                    batches(act, prologue, body, epilogue)

                @block.vector
                def _(dve):
                    def bank_of(*unit):
                        dve.wait_ge(shared_ready, shared.ready(*unit))
                        return banks[:, SHARED_BANK + shared.bank(*unit), :]

                    def norm_stats(w, b, sh):
                        k = norms("T" + w, b, sh)
                        if w == "":
                            if isinstance(b, int) and b + sh == 0:
                                dve.wait_ge(summed, tiles("Y1", 0, 0, 2))
                                dve.wait_ge(vector_summed, vector_tiles("Y1", 0, 0, 3))
                            else:
                                dve.wait_ge(summed, tiles("Y1", b, sh, QT - 1))
                            dve.memset(carrier[:, 0:1], 0.0)
                        if w == "2":
                            dve.wait_ge(shared_read_dve, shared.read["dve"]("O", b, sh, NPAIR // 2 - 1))
                            dve.memset(carrier[:, 0:1], 0.0)
                        for i in range(QT):
                            st_ = dve.bn_stats(stats[:, i, :], X[:, (b + sh) * QT + i, :])
                        st_.then_inc(stats_done, 1)
                        dve.wait_ge(stats_done, k)
                        dve.memset(carrier[:, 1:2], 0.0)
                        for i in range(QT):
                            st_ = dve.bn_aggr(meanvar[:, i, :], stats[:, i, :])
                        st_.then_inc(agg_done, 1)
                        dve.wait_ge(agg_done, k)
                        dve.tensor_scalar(var_eps[:, :], meanvar[:, :, 1], EPS, None, ALU.add).then_inc(eps_done, 1)

                    def norm_apply(w, b, sh):
                        dve.wait_ge(rstd_done, norms("T" + w, b, sh))
                        for i in range(QT):
                            st_ = dve.tensor_scalar(xn[:, i, :], X[:, (b + sh) * QT + i, :], meanvar[:, i, 0:1],
                                                    rstd[:, i:i + 1], ALU.subtract, ALU.mult)
                        st_.then_inc(xn_done, 1)

                    def low(w, b, sh):
                        o = bank_of("T" + w, b, sh)
                        dve.wait_ge(high_done, norms("T" + w, b, sh))
                        dve.tensor_tensor(xT_lo[w][:, :], o, xT_hi[w][:, :].bitcast(F32), ALU.subtract
                                          ).then_inc(shared_read_dve, 1)

                    def rank_experts(w, b, sh):
                        k = routes("L" + w, b, sh)
                        dve.wait_ge(shared_read_act, shared.read["act"]("L" + w, b, sh))
                        dve.tensor_reduce(top[:, :], logit[:, :, :], AX.X, ALU.max).then_inc(g_top, 1)
                        by_e = logit[:, :, :].unsqueeze(3).broadcast_to([P, QT, E, E])
                        by_j = logit[:, :, :].unsqueeze(2).broadcast_to([P, QT, E, E])
                        dve.tensor_tensor(ge[:, :, :, :], by_j, by_e, ALU.is_ge).then_inc(g_cmp, 1)
                        dve.wait_ge(g_top, k)
                        dve.tensor_tensor(shifted[:, :, :], logit[:, :, :],
                                          top[:, :].unsqueeze(2).broadcast_to([P, QT, E]),
                                          ALU.subtract).then_inc(shift_done, 1)
                        dve.wait_ge(g_cmp, k)
                        dve.tensor_tensor(ge[:, :, :, :].rearrange("p t e j -> p t (e j)"),
                                          ge[:, :, :, :].rearrange("p t e j -> p t (e j)"),
                                          earlier[:, :, :].rearrange("p e j -> p (e j)").unsqueeze(1).broadcast_to(
                                              [P, QT, E * E]), ALU.mult).then_inc(g_mul, 1)
                        dve.wait_ge(g_mul, k)
                        dve.tensor_reduce(row[:, :, :], ge[:, :, :, :], AX.X, ALU.add)
                        dve.tensor_reduce(col[:, :, :], ge[:, :, :, :].rearrange("p t e j -> p t j e"), AX.X,
                                          ALU.add).then_inc(g_rank, 1)
                        dve.wait_ge(g_rank, k)
                        dve.tensor_tensor(rank[:, :, :], row[:, :, :], col[:, :, :], ALU.subtract).then_inc(g_take, 1)
                        dve.wait_ge(g_take, k)
                        dve.tensor_tensor(taken[:, :, :], rank[:, :, :], rank_limit[:, :].unsqueeze(1).broadcast_to(
                            [P, QT, E]), ALU.is_lt).then_inc(g_add, 1)

                    def gates(w, b, sh):
                        k = routes("L" + w, b, sh)
                        dve.wait_ge(expo_done, k)
                        dve.tensor_reduce(total[:, :], expo[:, :, :], AX.X, ALU.add).then_inc(g_tot, 1)
                        dve.wait_ge(g_add, k)
                        dve.tensor_tensor(chosen[:, :, :], expo[:, :, :], taken[:, :, :], ALU.mult).then_inc(g_pick, 1)
                        dve.wait_ge(g_tot, k)
                        dve.tensor_scalar(twice[:, :], total[:, :], 1.0 / GATE_SCALE, None, ALU.mult).then_inc(g_twice, 1)
                        dve.wait_ge(g_twice, k)
                        dve.reciprocal(inv_total[:, :], twice[:, :]).then_inc(g_inv, 1)
                        dve.wait_ge(g_inv, k)
                        dve.wait_ge(g_pick, k)
                        dve.tensor_tensor(gate[w][:, :, :], chosen[:, :, :],
                                          inv_total[:, :].unsqueeze(2).broadcast_to([P, QT, E]),
                                          ALU.mult).then_inc(gate_done, 1)

                    def weigh_experts(w, b, sh, i, start, end):
                        if i == 0:
                            dve.wait_ge(gate_done, routes("L" + w, b, sh))
                        t, c = i // 2, i % 2
                        if c == 0 and start:
                            if t == 2:
                                dve.wait_ge(summed, tiles("Y1", 0, 0, 0))
                            if t == 3:
                                dve.wait_ge(vector_summed, vector_tiles("Y1", 0, 0, 1))
                        elif c == 0 and end:
                            if t < 2:
                                dve.wait_ge(summed, tiles("Y2", b, sh, 0, less=2 - t))
                            if t == 2:
                                dve.wait_ge(summed, tiles("Y2", b, sh, 0))
                            if t == 3:
                                dve.wait_ge(vector_summed, vector_tiles("Y2", b, sh, 1))
                        elif c == 0:
                            dve.wait_ge(summed, tiles("Y" + w, b, sh, t, less=2))
                        o = bank_of("Y" + w, b, sh, i)
                        es = slice(c * E // 2, (c + 1) * E // 2)
                        dve.tensor_tensor(Z[:, t % 2, es, :], o.rearrange("p (e d) -> p e d", d=D),
                                          gate[w][:, t, es].unsqueeze(2).broadcast_to([P, E // 2, D]),
                                          ALU.mult).then_inc(shared_read_dve, 1)

                    def add_up(w, b, sh, t):
                        k = vector_tiles("Y" + w, b, sh, t, less=1) * 3
                        z = Z[:, t % 2, :, :]
                        dve.wait_ge(shared_read_dve, shared.read["dve"]("Y" + w, b, sh, 2 * t + 1))
                        for n in (4, 2, 1):
                            if n < 4:
                                dve.wait_ge(vector_adds, k + (1 if n == 2 else 2))
                            dve.tensor_tensor(z[:, 0:n], z[:, 0:n], z[:, n:2 * n], ALU.add).then_inc(vector_adds, 1)
                        dve.wait_ge(vector_adds, k + 3)
                        x_t = X[:, (b + sh) * QT + t, :]
                        dve.tensor_tensor(x_t, x_t, z[:, 0], ALU.add).then_inc(vector_summed, 1)

                    def rotate(b, sh, p, n, start=False):
                        k, r = pair_no(b, sh, p), p % 2
                        o = bank_of("K" if n else "Q", b, sh, p)
                        if n == 0 and not start:
                            dve.wait_ge(low_done, k * 2 - 2)
                            dve.wait_ge(qk_done, k - 1)
                        dve.tensor_tensor(rot[:, r, n + 1, :], o, tables[:, n + 1, :], ALU.mult).then_inc(rotated, 1)
                        dve.tensor_tensor(rot[:, r, n, :], o, tables[:, n, :], ALU.mult).then_inc(shared_read_dve, 1)

                    def swap_halves(b, sh, p, n):
                        k, r = pair_no(b, sh, p), p % 2
                        dve.wait_ge(rotated, k * 2 + 1 + n // 2)
                        dve.memset(carrier[:, 2 + n // 2:3 + n // 2], 0.0)
                        swap = [(i + ROPE // 2) % ROPE for i in range(ROPE)]
                        dve.stream_shuffle(rot[:, r, n + 1, :], rot[:, r, n + 1, :], mask=swap).then_inc(turned_half, 1)

                    def maxima(b, h, units):
                        k = head_no(b, 0, h)
                        for u in units:
                            tiles_ = SCORE_UNITS[u]
                            dve.wait_ge(scores_ready, k * 3 + u + 1)
                            for i in tiles_:
                                at = SCORE_AT[i][1]
                                mx = dve.tensor_reduce(negmax[:, h % 2, i:i + 1], flat[:, at:at + (i + 1) * P],
                                                       AX.X, ALU.max, negate=True)
                            mx.then_inc(max_done, 1)

                    def invert(b, sh, p):
                        k = pair_no(b, sh, p)
                        dve.wait_ge(exp_done, k * 6 + 6)
                        dve.reciprocal(inv_den[:, :, :], den[:, p % 2, :, :]).then_inc(inv_done, 1)
                        dve.wait_ge(inv_done, k + 1)
                        dve.tensor_copy(inv_wide[:, :, :].rearrange("p i (a d) -> p i a d", a=2),
                                        inv_den[:, :, :].unsqueeze(3).broadcast_to([P, QT, 2, DK])).then_inc(wide_done, 1)

                    def normalise(b, sh, p, start=False):
                        dve.wait_ge(pv_ready, pair_no(b, sh, p) + 1)
                        dve.wait_ge(shared_read_act, shared.read["act"]("R", b, sh, p))
                        if p % 2 == 0 and not start:
                            dve.wait_ge(shared_ready, shared.ready("O", b, sh - 1, p // 2))
                        dve.tensor_tensor(OT[:, p, :], banks[:, O_BANK, :], R[:, :], ALU.mult).then_inc(o_done, 1)

                    def add_residual(b, sh, part):
                        o = bank_of("O", b, sh, part)
                        if part:
                            dve.wait_ge(shared_read_dve, shared.read["dve"]("O", b, sh, part - 1))
                        xb = X[:, bass.ds((b + sh) * QT, QT), :]
                        dve.tensor_tensor(xb, o.rearrange("p (t d) -> p t d", t=QT), xb, ALU.add).then_inc(shared_read_dve, 1)

                    def run(units, b, start=False, end=False):
                        for kind, sh, i in units:
                            if kind[0] == "T":
                                low(kind[1:], b, sh)
                            elif kind[0] == "Y":
                                weigh_experts(kind[1:], b, sh, i, start, end)
                                if (start or end) and i % 4 == 3:
                                    add_up(kind[1:], b, sh, i // 2)
                            elif kind == "O":
                                add_residual(b, sh, i)

                    def own(b, p, place, first, last):
                        for unit, sh in jobs(VECTOR, p, place, first, last):
                            {"S": norm_stats, "A": norm_apply, "G": rank_experts, "P": gates}[unit[0]](unit[1:], b, sh)

                    def prologue():
                        dve.memset(wrn, 0.0).then_inc(filled, 1)
                        dve.memset(minus_half[:, :], -0.5)
                        dve.memset(Q_lo[:, :, :, :].bitcast(F32), 0.0).then_inc(padded, 1)
                        dve.wait_ge(x_first_in, 16)
                        norm_stats("1", 0, 0)
                        norm_apply("1", 0, 0)
                        dve.wait_ge(hi_done, 1)
                        dve.tensor_tensor(Wr_lo[:, :], wrn, Wr_hi[:, :].bitcast(F32), ALU.subtract).then_inc(lo_done, 1)
                        for g in range(2):
                            dve.wait_ge(hi_done, 3 + g + 1)
                            cols = slice(g * BANK, (g + 1) * BANK)
                            dve.tensor_tensor(M_lo[:, cols], banks[:, M_BANK[g], :], M_hi[:, cols].bitcast(F32),
                                              ALU.subtract).then_inc(lo_done, 1)
                        for unit in FIRST:
                            g = unit[2]
                            if unit[0] == "W":
                                dve.wait_ge(hi_done, 5 + g + 1)
                                cols = slice((g % 2) * BANK, (g % 2 + 1) * BANK)
                                dve.tensor_tensor(W_lo[:, g // 2, cols], banks[:, W_BANK[g], :],
                                                  W_hi[:, g // 2, cols].bitcast(F32), ALU.subtract).then_inc(lo_done, 1)
                            elif unit[0] != "WO":
                                run([unit], 0, True)
                            if unit[0] == "T1":
                                dve.wait_ge(ident_in, 16)
                                dve.tensor_copy(ident_b[:, :], ident[:, :]).then_inc(cast, 1)
                                dve.wait_ge(mask_in, 16)
                                dve.tensor_copy(mask_b[:, :, :], mask_f.unsqueeze(1).broadcast_to([P, 2, P])).then_inc(cast, 1)
                            if unit[0] == "L1":
                                dve.wait_ge(rank_in, 32)
                                rank_experts("1", 0, 0)
                                gates("1", 0, 0)
                        norm_stats("", 0, 0)
                        norm_apply("", 0, 0)
                        run(THEN[:1], 0)
                        dve.wait_ge(tables_in, 64)
                        for p in range(2):
                            for n in (0, 2):
                                rotate(0, 0, p, n, True)
                            for n in (0, 2):
                                swap_halves(0, 0, p, n)
                        dve.wait_ge(x_in, 32)

                    def body(b, first, last):
                        for p in range(NPAIR):
                            sh, pp = before(p)
                            started = not (first and p == 0)
                            nsh, pn = after(p, 2)
                            more = not (last and nsh)
                            maxima(b, 2 * p, (0,))
                            own(b, p, "a", first, last)
                            maxima(b, 2 * p, (1, 2))
                            if started:
                                invert(b, sh, pp)
                            run(extras(p, "mid", first, last), b)
                            if more:
                                rotate(b, nsh, pn, 0)
                                rotate(b, nsh, pn, 2)
                            own(b, p, "b", first, last)
                            maxima(b, 2 * p + 1, (0,))
                            own(b, p, "c", first, last)
                            if started:
                                normalise(b, sh, pp, first)
                            own(b, p, "d", first, last)
                            maxima(b, 2 * p + 1, (1, 2))
                            run(extras(p, "end", first, last), b)
                            own(b, p, "e", first, last)
                            if more:
                                swap_halves(b, nsh, pn, 0)
                                swap_halves(b, nsh, pn, 2)
                            own(b, p, "f", first, last)
                            run(extras(p, "late", first, last), b)

                    def epilogue():
                        invert(B - 1, 0, NPAIR - 1)
                        normalise(B - 1, 0, NPAIR - 1)
                        run(EPILOGUE[:1], B - 1)
                        norm_stats("2", B - 1, 0)
                        norm_apply("2", B - 1, 0)
                        run(EPILOGUE[1:2], B - 1)
                        rank_experts("2", B - 1, 0)
                        gates("2", B - 1, 0)
                        run(EPILOGUE[2:], B - 1, end=True)

                    batches(dve, prologue, body, epilogue)

                @block.gpsimd
                def _(pool):
                    def norm_rstd(w, b, sh):
                        k = norms("T" + w, b, sh)
                        pool.wait_ge(eps_done, k)
                        pool.tensor_tensor(rstd[:, :], var_eps[:, :], minus_half[:, :], ALU.pow).then_inc(rstd_done, 1)
                        pool.wait_ge(rstd_done, k)

                    def sum_rotated(b, sh, p, n):
                        k, r = pair_no(b, sh, p), p % 2
                        pool.wait_ge(shared_read_dve, shared.read["dve"]("K" if n else "Q", b, sh, p))
                        pool.wait_ge(turned_half, k * 2 + n // 2 + 1)
                        pool.tensor_tensor(rot[:, r, n, :], rot[:, r, n, :], rot[:, r, n + 1, :], ALU.add).then_inc(qk_sum, 1)
                        pool.wait_ge(qk_sum, k * 2 + n // 2 + 1)

                    def low_k(b, sh, p, start=False):
                        k, r = pair_no(b, sh, p), p % 2
                        pool.wait_ge(qk_high, k * 3 + 1)
                        if not start:
                            pool.wait_ge(k_lo_moved, k * 2 * 16)
                        pool.tensor_tensor(K_lo[:, :], rot[:, r, 2, :], K_hi[:, :].bitcast(F32), ALU.subtract
                                           ).then_inc(low_done, 1)
                        pool.wait_ge(low_done, k * 2 + 1)

                    def low_q(b, sh, p):
                        k, r = pair_no(b, sh, p), p % 2
                        pool.wait_ge(qk_high, k * 3 + 2)
                        pool.tensor_tensor(Q_lo[OWN[0], r, 0, :], rot[OWN[0], r, 0, :], Q_hi[OWN[0], r, 0, :].bitcast(F32),
                                           ALU.subtract).then_inc(low_done, 1)
                        pool.wait_ge(qk_high, k * 3 + 3)
                        pool.wait_ge(low_done, k * 2 + 2)
                        pool.tensor_tensor(Q_lo[OWN[1], r, 1, :], rot[OWN[1], r, 0, :], Q_hi[OWN[1], r, 1, :].bitcast(F32),
                                           ALU.subtract).then_inc(qk_done, 1)
                        pool.wait_ge(qk_done, k + 1)

                    def add_up(w, b, sh, i):
                        k = tiles("Y" + w, b, sh, i, less=1) * 3
                        z = Z[:, i % 2, :, :]
                        pool.wait_ge(shared_read_dve, shared.read["dve"]("Y" + w, b, sh, 2 * i + 1))
                        pool.tensor_tensor(z[:, 0:4], z[:, 0:4], z[:, 4:8], ALU.add).then_inc(z_adds, 1)
                        pool.wait_ge(z_adds, k + 1)
                        pool.tensor_tensor(z[:, 0:2], z[:, 0:2], z[:, 2:4], ALU.add).then_inc(z_adds, 1)
                        pool.wait_ge(z_adds, k + 2)
                        pool.tensor_tensor(z[:, 0], z[:, 0], z[:, 1], ALU.add).then_inc(z_adds, 1)
                        pool.wait_ge(z_adds, k + 3)
                        x_t = X[:, (b + sh) * QT + i, :]
                        pool.tensor_tensor(x_t, x_t, z[:, 0], ALU.add).then_inc(summed, 1)
                        pool.wait_ge(summed, tiles("Y" + w, b, sh, i))

                    def run(units, b):
                        for kind, sh, i in units:
                            if kind[0] == "Y" and i % 2 and (kind, b + sh if isinstance(b, int) else None, i // 2) not in vector_sums:
                                add_up(kind[1:], b, sh, i // 2)

                    def roots(b, p, places, first, last):
                        for place in places:
                            for unit, sh in jobs(VECTOR, p, place, first, last):
                                if unit[0] == "S":
                                    norm_rstd(unit[1:], b, sh)

                    def prologue():
                        pool.wait_ge(padded, 1)
                        norm_rstd("1", 0, 0)
                        run(PROLOGUE, 0)
                        norm_rstd("", 0, 0)
                        sum_rotated(0, 0, 0, 0)
                        sum_rotated(0, 0, 0, 2)
                        low_k(0, 0, 0, True)
                        low_q(0, 0, 0)
                        sum_rotated(0, 0, 1, 0)
                        sum_rotated(0, 0, 1, 2)

                    def body(b, first, last):
                        for p in range(NPAIR):
                            nsh, pn = after(p, 1)
                            more = not (last and nsh)
                            n2, p2 = after(p, 2)
                            more2 = not (last and n2)
                            if more:
                                low_k(b, nsh, pn)
                            run(extras(p, "mid", first, last), b)
                            roots(b, p, "abcd", first, last)
                            if more:
                                low_q(b, nsh, pn)
                            if more2:
                                sum_rotated(b, n2, p2, 0)
                                sum_rotated(b, n2, p2, 2)
                            run(extras(p, "end", first, last), b)
                            roots(b, p, "ef", first, last)

                    def epilogue():
                        norm_rstd("2", B - 1, 0)
                        run(EPILOGUE, B - 1)

                    batches(pool, prologue, body, epilogue)

                @block.sync
                def _(sp):
                    sp.dma_start(ident[:, :], ident_d).then_inc(ident_in, 16)
                    sp.dma_start(woutn, w_out.rearrange("e h d -> h e d")).then_inc(wout_in, 16)
                    sp.wait_ge(filled, 1)
                    sp.dma_start(wrn[:, 0:E], w_r).then_inc(wr_in, 16)
                    sp.dma_start(earlier[:, :, :], rank_d[:, 0:E, :]).then_inc(rank_in, 16)
                    sp.dma_start(rank_limit[:, :], rank_d[:, E, :]).then_inc(rank_in, 16)
                    sp.dma_start(wn, w_qkv.rearrange("q h d m -> (q h d) m").rearrange("(t p) m -> p t m", p=P)
                                 ).then_inc(w_in, 16)
                    sp.dma_start(won, w_o).then_inc(wo_in, 16)
                    sp.dma_start(mask_f, mask_d).then_inc(mask_in, 16)
                    for n, t in enumerate((cos_q, sin_q, cos_k, sin_k)):
                        sp.dma_start(tables[:, n, :], t).then_inc(tables_in, 16)
                    half = B * QT // 2
                    sp.dma_start(X[:, QT:half, :], tokens[:, QT:half, :]).then_inc(x_in, 16)
                    sp.dma_start(X[:, half:, :], tokens[:, half:, :]).then_inc(x_in, 16)

                    o = out.rearrange("b (t p) d -> p b t d", p=P)

                    def store(b, sh):
                        if isinstance(b, int) and b + sh == B - 1:
                            sp.wait_ge(summed, tiles("Y2", b, sh, 2))
                            sp.wait_ge(vector_summed, vector_tiles("Y2", b, sh, 3))
                        else:
                            sp.wait_ge(summed, tiles("Y2", b, sh, QT - 1))
                        sp.dma_start(o[:, bass.ds(b + sh, 1), :, :], X[:, bass.ds((b + sh) * QT, QT), :].rearrange(
                            "p (a t) d -> p a t d", a=1)).then_inc(out_done, 16)

                    def place(b, sh, p):
                        k, r = pair_no(b, sh, p), p % 2
                        sp.wait_ge(qk_high, k * 3 + 1)
                        for a in range(2):
                            sp.dma_start(K_both[OWN[a], r, a, :].bitcast(F32), K_hi[OWN[a], :].bitcast(F32)).then_inc(k_hi_moved, 16)
                        sp.wait_ge(low_done, k * 2 + 1)
                        for a in range(2):
                            sp.dma_start(K_both[OWN[1 - a], r, a, :].bitcast(F32), K_lo[OWN[a], :].bitcast(F32)).then_inc(k_lo_moved, 16)
                        sp.wait_ge(qk_high, k * 3 + 3)
                        for a in range(2):
                            sp.dma_start(Q_hi[OWN[1 - a], r, a, :].bitcast(F32), Q_hi[OWN[a], r, a, :].bitcast(F32)).then_inc(q_moved, 16)

                    def body(b, first, last):
                        for p in range(NPAIR):
                            nsh, pn = after(p, 1)
                            if not (last and nsh):
                                place(b, nsh, pn)
                            if p == 1 and not first and not (isinstance(b, int) and b < 2):
                                store(b, -2)

                    place(0, 0, 0)
                    body(0, True, False)
                    body(1, False, False)
                    with sp.Fori(2, B - 1) as b:
                        body(b, False, False)
                    body(B - 1, False, True)
                    store(B - 1, -1)
                    store(B - 1, 0)
                    sp.wait_ge(out_done, 16 * B)


def shape_tables():
    inv_freq = (1.0 / np.power(np.float32(6000.0), np.arange(0, ROPE, 2, dtype=np.float32) / np.float32(ROPE))).astype(np.float32)
    angle = np.outer(np.arange(S, dtype=np.float32), inv_freq).astype(np.float32)
    cos, sin = np.cos(angle).astype(np.float32).T, np.sin(angle).astype(np.float32).T
    c = np.ones((DK, S), np.float32)
    s = np.zeros((DK, S), np.float32)
    c[0:16], c[16:32] = cos, cos
    s[0:16], s[16:32] = sin, -sin
    c, s = np.concatenate([c, c]), np.concatenate([s, s])
    scale = np.float32(1.0 / np.sqrt(DK))
    e = np.arange(E)
    rank = np.concatenate([e[None, :] < e[:, None], [TOPK - 0.5 - (E - 1 - e)]]).astype(np.float32)
    mask = np.where(np.arange(P)[None, :] > np.arange(P)[:, None], np.float32(-1e30), np.float32(0))
    return {
        "cos_q": c * scale, "sin_q": s * scale, "cos_k": c, "sin_k": s, "ident": np.eye(P, dtype=np.float32),
        "rank": np.ascontiguousarray(np.broadcast_to(rank, (P, E + 1, E))), "mask": mask.astype(np.float32),
    }


_INS = ['L0_attn_x', 'L0_attn_W_qkv', 'L0_attn_W_o', 'L0_ffn_Wr', 'L0_ffn_Wi', 'L0_ffn_Wo']


def kernel(**inputs):
    import concourse.bacc as _bacc
    from concourse.bass_utils import run_bass_kernel_spmd as _run

    nc = _bacc.Bacc("TRN2", target_bir_lowering=False, num_devices=1)
    arrays, args = {}, []
    for name, a in [(n, inputs[n]) for n in _INS] + list(shape_tables().items()):
        a = np.ascontiguousarray(a)
        arrays[f"in_{name}_dram"] = a
        args.append(nc.dram_tensor(f"in_{name}_dram", a.shape, mybir.dt.from_np(a.dtype), kind="ExternalInput").ap())
    args.append(nc.dram_tensor("out_dram", (B, S, D), F32, kind="ExternalOutput").ap())
    build(nc, *args)
    r = _run(nc, [arrays], core_ids=[0])
    return r.results[0]["out_dram"]
```
